# Optimizing a Trainium2 kernel written in Bass

```python
import numpy as np
import jax
import jax.numpy as jnp

def _softmax(x, axis=-1):
    return jax.nn.softmax(x, axis=axis)

def _gelu(x):
    return jax.nn.gelu(x, approximate=True)

def _silu(x):
    return jax.nn.silu(x)

def _sigmoid(x):
    return jax.nn.sigmoid(x)

def _layernorm(x, axis=-1, eps=1e-05):
    m = jnp.mean(x, axis=axis, keepdims=True)
    v = jnp.var(x, axis=axis, keepdims=True)
    return (x - m) / jnp.sqrt(v + eps)

def _scatter_add(tgt, idx, src, axis=0):
    return tgt.at[idx].add(src)

def _segment_sum(src, seg, n):
    return jax.ops.segment_sum(src, seg, n)
kernel_name = 'mk_prb_d1_jaxref_r8_32e235'

def setup_inputs(seed: int=0):
    np.random.seed(seed)
    _w = jnp.asarray

    def _L0_attn_setup():
        import jax, jax.numpy as jnp
        import numpy as np
        L, E, H = (4, 128, 16)
        HD = E // H
        EPS_LN = 1e-05

        def _layernorm(x, w, b):
            m = jnp.mean(x, axis=-1, keepdims=True)
            v = jnp.mean((x - m) ** 2, axis=-1, keepdims=True)
            return (x - m) / jnp.sqrt(v + EPS_LN) * w + b

        def _to_quaternion(x):
            p1 = jnp.diff(x, axis=1, prepend=x[:, :1])
            p2 = jnp.roll(x, 1, axis=2)
            p3 = jnp.cos(x)
            return jnp.stack([x, p1, p2, p3], axis=-1)

        def _hamilton(a, b):
            a0, a1, a2, a3 = (a[..., 0], a[..., 1], a[..., 2], a[..., 3])
            b0, b1, b2, b3 = (b[..., 0], b[..., 1], b[..., 2], b[..., 3])
            return jnp.stack([a0 * b0 - a1 * b1 - a2 * b2 - a3 * b3, a0 * b1 + a1 * b0 + a2 * b3 - a3 * b2, a0 * b2 - a1 * b3 + a2 * b0 + a3 * b1, a0 * b3 + a1 * b2 - a2 * b1 + a3 * b0], axis=-1)

        def _spectral_filter(S):
            ks = jnp.fft.fftfreq(S).astype(jnp.float32)[:, None, None]
            kh = jnp.fft.fftfreq(H).astype(jnp.float32)[None, :, None]
            kd = jnp.fft.fftfreq(HD).astype(jnp.float32)[None, None, :]
            km = jnp.sqrt(ks ** 2 + kh ** 2 + kd ** 2 + 1e-10)
            f = jnp.exp(1j * jnp.arctan(jnp.log(km + 1e-10)))
            return f[None, :, :, :, None].astype(jnp.complex64)

        def _modulation(S):
            lam = jnp.arange(S, dtype=jnp.float32) / S
            t = jnp.arange(S, dtype=jnp.float32) * 0.1
            probe = jnp.sin(t + lam)
            phase = t - 2.0 * lam + 0.5 * lam ** 2
            return (probe * jnp.cos(phase))[None, :, None, None]

        def _attention(x, aw, ab, pw, pb):
            B, S, _ = x.shape
            qkv = (x @ aw + ab).reshape(B, S, H, 3 * HD)
            q, k, v = jnp.split(qkv, 3, axis=-1)
            qk = _hamilton(_to_quaternion(q), _to_quaternion(k))
            qkv_p = _hamilton(qk, _to_quaternion(v))
            f = jnp.fft.fftn(qkv_p.astype(jnp.complex64), axes=(-3, -2))
            out = jnp.fft.ifftn(f * _spectral_filter(S), axes=(-3, -2)).real
            a = out[..., 0] * (1.0 + 0.1 * _modulation(S))
            return a.reshape(B, S, E) @ pw + pb

        def _layer(x, p):
            ln1w, ln1b, aw, ab, pw, pb, ln2w, ln2b, fw, fb, mw, mb = p
            x = x + _attention(_layernorm(x, ln1w, ln1b), aw, ab, pw, pb)
            h = _layernorm(x, ln2w, ln2b)
            h = jax.nn.gelu(h @ fw + fb, approximate=False) @ mw + mb
            return x + h
        key = jax.random.key(seed)
        ks = jax.random.split(key, 6)
        s = 0.02
        return {'x': jax.random.normal(ks[0], (2, 256, E), jnp.float32), 'ln1_w': jnp.ones((L, E), jnp.float32), 'ln1_b': jnp.zeros((L, E), jnp.float32), 'attn_w': jax.random.normal(ks[1], (L, E, 3 * E), jnp.float32) * s, 'attn_b': jnp.zeros((L, 3 * E), jnp.float32), 'aproj_w': jax.random.normal(ks[2], (L, E, E), jnp.float32) * s, 'aproj_b': jnp.zeros((L, E), jnp.float32), 'ln2_w': jnp.ones((L, E), jnp.float32), 'ln2_b': jnp.zeros((L, E), jnp.float32), 'fc_w': jax.random.normal(ks[3], (L, E, 4 * E), jnp.float32) * s, 'fc_b': jnp.zeros((L, 4 * E), jnp.float32), 'mproj_w': jax.random.normal(ks[4], (L, 4 * E, E), jnp.float32) * s, 'mproj_b': jnp.zeros((L, E), jnp.float32)}
    _L0_attn_in = _L0_attn_setup()

    def _L0_ffn_setup():
        import jax, jax.numpy as jnp
        import numpy as np
        B, L, C1, C2, K, K_IN = (4, 128, 128, 128, 32, 32)
        BN_EPS = 1e-05

        def _gated_bottleneck(x2d, conv_w, conv_b, gamma, beta, lin_w, lin_b):
            n = x2d.shape[0]
            g = conv_w.shape[0]
            xc = jnp.einsum('ngf,gf->ng', x2d.reshape(n, g, 4), conv_w) + conv_b
            mean = jnp.mean(xc, axis=0)
            var = jnp.mean((xc - mean) ** 2, axis=0)
            xn = (xc - mean) * jax.lax.rsqrt(var + BN_EPS) * gamma + beta
            xa = jax.nn.gelu(xn, approximate=False)
            return xa @ lin_w.T + lin_b
        key = jax.random.key(seed)
        ks = jax.random.split(key, 8)
        g = C1 // 4
        w_std = (2.0 / C2) ** 0.5
        lin_std = (1.0 / g) ** 0.5
        return {'x': jax.random.normal(ks[0], (B, L, C1), jnp.float32), 'weight': jax.random.normal(ks[1], (C1, C2), jnp.float32) * w_std, 'bias': jnp.zeros((C2,), jnp.float32), 'so_conv_w': jax.random.normal(ks[2], (g, 4), jnp.float32) * 0.5, 'so_conv_b': jnp.zeros((g,), jnp.float32), 'so_gamma': jnp.ones((g,), jnp.float32), 'so_beta': jnp.zeros((g,), jnp.float32), 'so_lin_w': jax.random.normal(ks[3], (C2, g), jnp.float32) * lin_std, 'so_lin_b': jnp.zeros((C2,), jnp.float32), 'si_conv_w': jax.random.normal(ks[4], (g, 4), jnp.float32) * 0.5, 'si_conv_b': jnp.zeros((g,), jnp.float32), 'si_gamma': jnp.ones((g,), jnp.float32), 'si_beta': jnp.zeros((g,), jnp.float32), 'si_lin_w': jax.random.normal(ks[5], (C1, g), jnp.float32) * lin_std, 'si_lin_b': jnp.zeros((C1,), jnp.float32)}
    _L0_ffn_in = _L0_ffn_setup()
    _d = {'L0_attn_x': _L0_attn_in['x'], 'L0_attn_ln1_w': _L0_attn_in['ln1_w'], 'L0_attn_ln1_b': _L0_attn_in['ln1_b'], 'L0_attn_attn_w': _L0_attn_in['attn_w'], 'L0_attn_attn_b': _L0_attn_in['attn_b'], 'L0_attn_aproj_w': _L0_attn_in['aproj_w'], 'L0_attn_aproj_b': _L0_attn_in['aproj_b'], 'L0_attn_ln2_w': _L0_attn_in['ln2_w'], 'L0_attn_ln2_b': _L0_attn_in['ln2_b'], 'L0_attn_fc_w': _L0_attn_in['fc_w'], 'L0_attn_fc_b': _L0_attn_in['fc_b'], 'L0_attn_mproj_w': _L0_attn_in['mproj_w'], 'L0_attn_mproj_b': _L0_attn_in['mproj_b'], 'L0_ffn_weight': _L0_ffn_in['weight'], 'L0_ffn_bias': _L0_ffn_in['bias'], 'L0_ffn_so_conv_w': _L0_ffn_in['so_conv_w'], 'L0_ffn_so_conv_b': _L0_ffn_in['so_conv_b'], 'L0_ffn_so_gamma': _L0_ffn_in['so_gamma'], 'L0_ffn_so_beta': _L0_ffn_in['so_beta'], 'L0_ffn_so_lin_w': _L0_ffn_in['so_lin_w'], 'L0_ffn_so_lin_b': _L0_ffn_in['so_lin_b'], 'L0_ffn_si_conv_w': _L0_ffn_in['si_conv_w'], 'L0_ffn_si_conv_b': _L0_ffn_in['si_conv_b'], 'L0_ffn_si_gamma': _L0_ffn_in['si_gamma'], 'L0_ffn_si_beta': _L0_ffn_in['si_beta'], 'L0_ffn_si_lin_w': _L0_ffn_in['si_lin_w'], 'L0_ffn_si_lin_b': _L0_ffn_in['si_lin_b']}
    _x0 = _d['L0_attn_x']
    _d['L0_attn_x'] = jax.random.normal(jax.random.fold_in(jax.random.key(seed), 1), (4, 512, 128), dtype=_x0.dtype)
    del _x0
    return _d

def reference(L0_attn_x, L0_attn_ln1_w, L0_attn_ln1_b, L0_attn_attn_w, L0_attn_attn_b, L0_attn_aproj_w, L0_attn_aproj_b, L0_attn_ln2_w, L0_attn_ln2_b, L0_attn_fc_w, L0_attn_fc_b, L0_attn_mproj_w, L0_attn_mproj_b, L0_ffn_weight, L0_ffn_bias, L0_ffn_so_conv_w, L0_ffn_so_conv_b, L0_ffn_so_gamma, L0_ffn_so_beta, L0_ffn_so_lin_w, L0_ffn_so_lin_b, L0_ffn_si_conv_w, L0_ffn_si_conv_b, L0_ffn_si_gamma, L0_ffn_si_beta, L0_ffn_si_lin_w, L0_ffn_si_lin_b):

    def _L0_attn_ref(x, ln1_w, ln1_b, attn_w, attn_b, aproj_w, aproj_b, ln2_w, ln2_b, fc_w, fc_b, mproj_w, mproj_b):
        import jax, jax.numpy as jnp
        import numpy as np
        L, E, H = (4, 128, 16)
        HD = E // H
        EPS_LN = 1e-05

        def _layernorm(x, w, b):
            m = jnp.mean(x, axis=-1, keepdims=True)
            v = jnp.mean((x - m) ** 2, axis=-1, keepdims=True)
            return (x - m) / jnp.sqrt(v + EPS_LN) * w + b

        def _to_quaternion(x):
            p1 = jnp.diff(x, axis=1, prepend=x[:, :1])
            p2 = jnp.roll(x, 1, axis=2)
            p3 = jnp.cos(x)
            return jnp.stack([x, p1, p2, p3], axis=-1)

        def _hamilton(a, b):
            a0, a1, a2, a3 = (a[..., 0], a[..., 1], a[..., 2], a[..., 3])
            b0, b1, b2, b3 = (b[..., 0], b[..., 1], b[..., 2], b[..., 3])
            return jnp.stack([a0 * b0 - a1 * b1 - a2 * b2 - a3 * b3, a0 * b1 + a1 * b0 + a2 * b3 - a3 * b2, a0 * b2 - a1 * b3 + a2 * b0 + a3 * b1, a0 * b3 + a1 * b2 - a2 * b1 + a3 * b0], axis=-1)

        def _spectral_filter(S):
            ks = jnp.fft.fftfreq(S).astype(jnp.float32)[:, None, None]
            kh = jnp.fft.fftfreq(H).astype(jnp.float32)[None, :, None]
            kd = jnp.fft.fftfreq(HD).astype(jnp.float32)[None, None, :]
            km = jnp.sqrt(ks ** 2 + kh ** 2 + kd ** 2 + 1e-10)
            f = jnp.exp(1j * jnp.arctan(jnp.log(km + 1e-10)))
            return f[None, :, :, :, None].astype(jnp.complex64)

        def _modulation(S):
            lam = jnp.arange(S, dtype=jnp.float32) / S
            t = jnp.arange(S, dtype=jnp.float32) * 0.1
            probe = jnp.sin(t + lam)
            phase = t - 2.0 * lam + 0.5 * lam ** 2
            return (probe * jnp.cos(phase))[None, :, None, None]

        def _attention(x, aw, ab, pw, pb):
            B, S, _ = x.shape
            qkv = (x @ aw + ab).reshape(B, S, H, 3 * HD)
            q, k, v = jnp.split(qkv, 3, axis=-1)
            qk = _hamilton(_to_quaternion(q), _to_quaternion(k))
            qkv_p = _hamilton(qk, _to_quaternion(v))
            f = jnp.fft.fftn(qkv_p.astype(jnp.complex64), axes=(-3, -2))
            out = jnp.fft.ifftn(f * _spectral_filter(S), axes=(-3, -2)).real
            a = out[..., 0] * (1.0 + 0.1 * _modulation(S))
            return a.reshape(B, S, E) @ pw + pb

        def _layer(x, p):
            ln1w, ln1b, aw, ab, pw, pb, ln2w, ln2b, fw, fb, mw, mb = p
            x = x + _attention(_layernorm(x, ln1w, ln1b), aw, ab, pw, pb)
            h = _layernorm(x, ln2w, ln2b)
            h = jax.nn.gelu(h @ fw + fb, approximate=False) @ mw + mb
            return x + h
        for i in range(L):
            x = _layer(x, (ln1_w[i], ln1_b[i], attn_w[i], attn_b[i], aproj_w[i], aproj_b[i], ln2_w[i], ln2_b[i], fc_w[i], fc_b[i], mproj_w[i], mproj_b[i]))
        return x

    def _L0_ffn_ref(x, weight, bias, so_conv_w, so_conv_b, so_gamma, so_beta, so_lin_w, so_lin_b, si_conv_w, si_conv_b, si_gamma, si_beta, si_lin_w, si_lin_b):
        import jax, jax.numpy as jnp
        import numpy as np
        B, L, C1, C2, K, K_IN = (4, 128, 128, 128, 32, 32)
        BN_EPS = 1e-05

        def _gated_bottleneck(x2d, conv_w, conv_b, gamma, beta, lin_w, lin_b):
            n = x2d.shape[0]
            g = conv_w.shape[0]
            xc = jnp.einsum('ngf,gf->ng', x2d.reshape(n, g, 4), conv_w) + conv_b
            mean = jnp.mean(xc, axis=0)
            var = jnp.mean((xc - mean) ** 2, axis=0)
            xn = (xc - mean) * jax.lax.rsqrt(var + BN_EPS) * gamma + beta
            xa = jax.nn.gelu(xn, approximate=False)
            return xa @ lin_w.T + lin_b
        b, l, c1 = x.shape
        c2 = weight.shape[1]
        x2d = x.reshape(b * l, c1)
        bi = jnp.arange(b)[:, None, None]
        li = jnp.arange(l)[None, :, None]
        score_out = jax.nn.softmax(_gated_bottleneck(x2d, so_conv_w, so_conv_b, so_gamma, so_beta, so_lin_w, so_lin_b).reshape(b, l, c2), axis=-1)
        s_v_out, s_i_out = jax.lax.top_k(score_out, K)
        full = jnp.einsum('blc,co->blo', x, weight)
        out_k = jnp.take_along_axis(full, s_i_out, axis=-1) * s_v_out
        out_branch = jnp.zeros((b, l, c2), x.dtype).at[bi, li, s_i_out].add(out_k)
        score_in = jax.nn.softmax(_gated_bottleneck(x2d, si_conv_w, si_conv_b, si_gamma, si_beta, si_lin_w, si_lin_b).reshape(b, l, c1), axis=-1)
        s_v_in, s_i_in = jax.lax.top_k(score_in, K_IN)
        x_gated = jnp.take_along_axis(x, s_i_in, axis=-1) * s_v_in
        x_sparse = jnp.zeros((b, l, c1), x.dtype).at[bi, li, s_i_in].add(x_gated)
        in_branch = jnp.einsum('blc,co->blo', x_sparse, weight)
        return out_branch + in_branch + bias
    x = L0_attn_x
    xn = _layernorm(x, axis=-1)
    x = x + _L0_attn_ref(xn, L0_attn_ln1_w, L0_attn_ln1_b, L0_attn_attn_w, L0_attn_attn_b, L0_attn_aproj_w, L0_attn_aproj_b, L0_attn_ln2_w, L0_attn_ln2_b, L0_attn_fc_w, L0_attn_fc_b, L0_attn_mproj_w, L0_attn_mproj_b) + _L0_ffn_ref(xn, L0_ffn_weight, L0_ffn_bias, L0_ffn_so_conv_w, L0_ffn_so_conv_b, L0_ffn_so_gamma, L0_ffn_so_beta, L0_ffn_so_lin_w, L0_ffn_so_lin_b, L0_ffn_si_conv_w, L0_ffn_si_conv_b, L0_ffn_si_gamma, L0_ffn_si_beta, L0_ffn_si_lin_w, L0_ffn_si_lin_b)
    return x

_drawn_inputs = setup_inputs


def setup_inputs(seed=0):
    import zlib

    import numpy as np

    out = dict(_drawn_inputs(seed))
    spreads = {'L0_attn_ln1_w': (1.0, 0.6),
     'L0_attn_ln1_b': (0.0, 0.8),
     'L0_attn_attn_b': (0.0, 0.1),
     'L0_attn_aproj_b': (0.0, 0.1),
     'L0_attn_ln2_w': (1.0, 0.6),
     'L0_attn_ln2_b': (0.0, 0.8),
     'L0_attn_fc_b': (0.0, 0.331),
     'L0_attn_mproj_b': (0.0, 0.1),
     'L0_ffn_bias': (0.0, 0.1),
     'L0_ffn_so_conv_b': (0.0, 0.8),
     'L0_ffn_so_gamma': (1.0, 0.6),
     'L0_ffn_so_beta': (0.0, 0.8),
     'L0_ffn_so_lin_b': (0.0, 0.8),
     'L0_ffn_si_conv_b': (0.0, 0.8),
     'L0_ffn_si_gamma': (1.0, 0.6),
     'L0_ffn_si_beta': (0.0, 0.8),
     'L0_ffn_si_lin_b': (0.0, 0.8)}
    factors = {'L0_ffn_weight': 6.274,
     'L0_ffn_so_conv_w': 8.0,
     'L0_ffn_so_lin_w': 8.0,
     'L0_ffn_si_conv_w': 8.0,
     'L0_ffn_si_lin_w': 8.0}
    for name, (base, spread) in spreads.items():
        noise = np.random.default_rng([zlib.crc32(name.encode()), seed]).standard_normal(out[name].shape)
        drawn = base * np.exp(spread * noise) if base else spread * noise
        out[name] = jnp.asarray(drawn.astype(out[name].dtype))
    for name, factor in factors.items():
        out[name] = (out[name] * factor).astype(out[name].dtype)
    return out
```

```python
from contextlib import ExitStack

import numpy as np

import concourse.bass as bass
from concourse import mybir

F32 = mybir.dt.float32
ALU = mybir.AluOpType
ACT = mybir.ActivationFunctionType

P = 128
B, S, E = 4, 512, 128
H, HD = 16, 8
LAYERS = 4
T = S // P
NT = B * T
FF = 4 * E
FK = FF // P
G = E // 4
TOPK = 32
EPS = 1e-5
TURN = 6.283185
INV_TURN = 1.0 / (2.0 * np.pi)
ROUND = 12582912.0
SELECTED = -3.0e38
NPAR = 11
LN1W, LN1B, QKVB, LN2W, LN2B, FCB = 0, 1, 2, 5, 6, 7
C_R, C_ID, C_GAIN, C_GROUP = 0, 128, 256, 768
NCONST = C_GROUP + G


def shape_constants():
    def cas(n):
        a = 2.0 * np.pi * np.outer(np.arange(n), np.arange(n)) / n
        return np.cos(a) + np.sin(a)
    c = np.zeros((P, NCONST), np.float64)
    c[:, C_R:C_R + E] = np.kron(cas(H), cas(HD)) / np.sqrt(E)
    c[:, C_ID:C_ID + P] = np.eye(P)
    kh = np.fft.fftfreq(H)[:, None, None]
    kd = np.fft.fftfreq(HD)[None, :, None]
    ks = np.fft.fftfreq(S)[None, None, :]
    km = np.sqrt(ks ** 2 + kh ** 2 + kd ** 2 + 1e-10)
    gain = np.cos(np.arctan(np.log(km + 1e-10))).reshape(E, S)
    lam = np.arange(S) / S
    t = np.arange(S) * 0.1
    mod = np.sin(t + lam) * np.cos(t - 2.0 * lam + 0.5 * lam ** 2)
    c[:, C_GAIN:C_GAIN + S] = gain * (1.0 + 0.1 * mod)
    c[:, C_GROUP:C_GROUP + G] = (np.arange(P)[:, None] // 4 == np.arange(G)[None, :])
    return c.astype(np.float32)


class Turn:

    def __init__(self, layer, k):
        self.layer = layer + k // B if isinstance(layer, int) or k >= B else layer
        self.base, self.k = layer, k
        self.b = k % B
        self.par = k % 2
        self.tiles = slice(T * self.b, T * self.b + T)

    def count(self, per=1, plus=0):
        return self.base * (B * per) + (self.k * per + plus)

    def pairs(self, per, plus=0):
        return self.base * (B // 2 * per) + (self.k // 2 * per + plus)


def build(nc, t, consts, out):
    with ExitStack() as ctx:
        def sb(name, shape, dt=F32):
            return ctx.enter_context(nc.sbuf_tensor(name, shape, dt))

        def psum(name, shape):
            return ctx.enter_context(nc.psum_tensor(name, shape, F32))

        def sem(name):
            return ctx.enter_context(nc.semaphore(name))

        const = sb("const", [P, NCONST])
        hartley = const[:, C_R:C_R + E]
        ident = const[:, C_ID:C_ID + P]
        gain = const[:, C_GAIN:C_GAIN + S]
        group = const[:, C_GROUP:C_GROUP + G]
        neg_hartley = sb("neg_hartley", [P, E])
        ones_row = sb("ones_row", [P, P])
        pause = sb("pause", [P, 1])
        eps_tile = sb("eps_tile", [P, T])
        minus_half = sb("minus_half", [P, NT])
        x_in = sb("x_in", [P, NT, E])
        x_stream = sb("x_stream", [P, NT, E])
        acc = sb("acc", [P, NT, E])
        par_rows = sb("par_rows", [LAYERS * NPAR, P])
        par_all = sb("par_all", [P, LAYERS * NPAR])
        par_pre = sb("par_pre", [P, LN2W])
        par_post = sb("par_post", [P, NPAR - LN2W])
        out_bias = sb("out_bias", [P, 2, LAYERS * E])
        w_qkv_raw = sb("w_qkv_raw", [P, 3 * E])
        w_qkv = sb("w_qkv", [P, 3, E])
        w_fc = sb("w_fc", [P, FF])
        w_mlp = sb("w_mlp", [P, LAYERS * FK * E])
        w_proj = sb("w_proj", [P, LAYERS * E])
        w_rproj = sb("w_rproj", [P, LAYERS * E])
        stats0 = sb("stats0", [P, NT, 6])
        stats1 = sb("stats1", [P, NT, 6])
        stats2 = sb("stats2", [P, NT, 6])
        meanvar0 = sb("meanvar0", [P, NT, 2])
        var_eps0 = sb("var_eps0", [P, NT])
        rstd0 = sb("rstd0", [P, NT])
        meanvar = sb("meanvar", [P, 2, NT, 2])
        var_eps = sb("var_eps", [P, 2, NT])
        rstd = sb("rstd", [P, 2, NT])
        normed = sb("normed", [P, 2, T, E])
        h1 = sb("h1", [P, S])
        h2 = sb("h2", [P, S])
        quat = sb("quat", [P, 2, 4, 3, S])
        turns = sb("turns", [P, 3, S])
        frac = sb("frac", [P, 3, S])
        square = sb("square", [P, 4, S])
        four_p = sb("four_p", [P, 4, S])
        triple = sb("triple", [P, 4, S])
        dprod = sb("dprod", [P, S])
        prod_a = sb("prod_a", [P, 2, S])
        prod_b = sb("prod_b", [P, 2, S])
        prod_c = sb("prod_c", [P, 2, S])
        cross_a = sb("cross_a", [P, 2, S])
        cross_b = sb("cross_b", [P, 2, S])
        filtered = sb("filtered", [P, S])
        hidden = sb("hidden", [P, FK, S])
        result = sb("result", [P, 2, T, E])
        xT = hidden
        conv_col = sb("conv_col", [P, 2])
        w_conv = sb("w_conv", [P, 2 * G])
        bott = sb("bott", [2 * G, 4])
        conv_out = triple[0:2 * G]
        gate = four_p[0:2 * G + 1]
        lin_rows = sb("lin_rows", [P, 2 * G])
        w_lin = sb("w_lin", [2 * G + 1, 2 * E])
        w_ffn = sb("w_ffn", [P, E])
        ffn_bias = sb("ffn_bias", [P, E])
        bn_stats = sb("bn_stats", [2 * G, B, 6])
        bn_mv = sb("bn_mv", [2 * G, 2])
        bn_sc = sb("bn_sc", [2 * G, 4])
        top = sb("top", [P, 2, 2, 8])
        logits = sb("logits", [P, 2, 2, E])
        left = sb("left", [P, 2, 2, E])
        neg_max = sb("neg_max", [P, 2, 2])
        expd = sb("expd", [P, 2, 2, E])
        esum = sb("esum", [P, 2, 2])
        rsum = sb("rsum", [P, 2, 2])
        kept = sb("kept", [P, 2, 2, E])
        branch = sb("branch", [P, 2, E])
        branch_x = sb("branch_x", [P, 2, E])
        sparse = sb("sparse", [P, 2, E])
        sparseT = sb("sparseT", [P, 2, E])

        ps_t = psum("ps_t", [P, S])
        ps_qkv = psum("ps_qkv", [P, 3, S])
        ps_spec = psum("ps_spec", [P, S])
        ps_out = psum("ps_out", [P, S])
        ps_fc = psum("ps_fc", [P, 2, S])

        s = {name: sem(name) for name in (
            "x0_in x1_in x2_in x3_in const_in par_in wproj_in wqkv_in wqkv_sb wfc_in wmlp_in obias_in conv_in lin_in "
            "bott_in ffnw_in linb_in out0_out out1_out rolled0 rolled1 "
            "const_made zeroed neg_made par_ps par_sb rproj_ps rproj_sb convw_made linT_ps linT_sb gate_ones "
            "s0_raw s0_mv s0_eps s0_rstd x0_ready xt_ps xt_sb conv_ps conv_sb bn_raw bn_mv_r bn_eps_r bn_rstd "
            "bn_scale_r bn_ms_r bn_shift gated logits_ps logits_sb full_ps topped negmax_r exped rsum_r kept_r branched "
            "sparsed branch_xed sparse_ps sparse_sb in_ps acc_made m8_r mr_r "
            "ln1_raw ln1_stats ln1_eps ln1_rstd ln1_norm t1_ps h1_sb qkv_ps qkv_sb diffed turned rounded fraced "
            "cosined par_pre_r par_post_r "
            "squared d_r u_r c0_r c1a_r zy_r zz_r c1_r pa_r pb_r pc_r c23_r crossa_r crossed tripled "
            "spec_ps filter_sb attn_ps x_mid ln2_raw ln2_stats ln2_eps ln2_rstd ln2_norm t2_ps h2_sb fc_ps "
            "gelued mlp_ps x_ready acc_mid resulted"
        ).split()}

        tiled = lambda ap: ap.rearrange("(b t p) e -> b p t e", t=T, p=P)
        x_dram = tiled(t["L0_attn_x"].rearrange("b s e -> (b s) e"))
        out_dram = tiled(out.rearrange("b s e -> (b s) e"))
        qkv_w_dram = t["L0_attn_attn_w"]
        fc_w_dram = t["L0_attn_fc_w"]

        block = ctx.enter_context(nc.Block())

        @block.sync
        def _(sp):
            for b in range(B):
                sp.dma_start(x_in[:, T * b:T * b + T, :], x_dram[b]).then_inc(s[f"x{b}_in"], 16)
                if b == 0:
                    sp.dma_start(const[:, :], consts).then_inc(s["const_in"], 16)
            for row, name in ((LN1W, "ln1_w"), (LN1B, "ln1_b"), (LN2W, "ln2_w"), (LN2B, "ln2_b")):
                sp.dma_start(par_rows[row:row + NPAR * (LAYERS - 1) + 1:NPAR, :],
                             t["L0_attn_" + name]).then_inc(s["par_in"], 16)
            for j in range(3):
                sp.dma_start(
                    par_rows[QKVB + j:QKVB + j + NPAR * (LAYERS - 1) + 1:NPAR, :].rearrange("l (h d) -> l h d", d=HD),
                    t["L0_attn_attn_b"].rearrange("l (h j d) -> j l h d", j=3, d=HD)[j]).then_inc(s["par_in"], 16)
            for k in range(FK):
                sp.dma_start(par_rows[FCB + k:FCB + k + NPAR * (LAYERS - 1) + 1:NPAR, :],
                             t["L0_attn_fc_b"][:, k * P:(k + 1) * P]).then_inc(s["par_in"], 16)
            sp.dma_start(w_qkv_raw[:, :], qkv_w_dram[0]).then_inc(s["wqkv_in"], 16)
            for g, name in enumerate(("so", "si")):
                sp.dma_start(conv_col[:, g:g + 1],
                             t[f"L0_ffn_{name}_conv_w"].rearrange("g (f o) -> (g f) o", o=1)).then_inc(s["conv_in"], 16)
                for c, vec in enumerate(("conv_b", "gamma", "beta")):
                    sp.dma_start(bott[g * G:(g + 1) * G, c:c + 1],
                                 t[f"L0_ffn_{name}_{vec}"].rearrange("(g o) -> g o", o=1)).then_inc(s["bott_in"], 16)
                sp.dma_start(lin_rows[:, g * G:(g + 1) * G], t[f"L0_ffn_{name}_lin_w"]).then_inc(s["lin_in"], 16)
            sp.dma_start(w_ffn[:, :], t["L0_ffn_weight"]).then_inc(s["ffnw_in"], 16)
            sp.wait_ge(s["gate_ones"], 1)
            sp.dma_start(ffn_bias[0:1, :], t["L0_ffn_bias"].rearrange("(o e) -> o e", o=1)).then_inc(s["ffnw_in"], 16)
            for g, name in enumerate(("so", "si")):
                sp.dma_start(w_lin[2 * G:2 * G + 1, g * E:(g + 1) * E],
                             t[f"L0_ffn_{name}_lin_b"].rearrange("(o e) -> o e", o=1)).then_inc(s["linb_in"], 16)
            sp.dma_start(w_proj[:, :].rearrange("p (l e) -> p l e", l=LAYERS),
                         t["L0_attn_aproj_w"].rearrange("l i e -> i l e")).then_inc(s["wproj_in"], 16)
            sp.dma_start(out_bias[0:1, 0, :], t["L0_attn_aproj_b"].rearrange("(o l) e -> o (l e)", o=1)).then_inc(s["obias_in"], 16)
            sp.dma_start(out_bias[0:1, 1, :], t["L0_attn_mproj_b"].rearrange("(o l) e -> o (l e)", o=1)).then_inc(s["obias_in"], 16)
            sp.dma_start(w_fc[:, :], fc_w_dram[0]).then_inc(s["wfc_in"], 16)
            sp.dma_start(w_mlp[:, :].rearrange("p (l k e) -> p l k e", l=LAYERS, k=FK),
                         t["L0_attn_mproj_w"].rearrange("l (k p) e -> p l k e", p=P)).then_inc(s["wmlp_in"], 16)

            def roll(n):
                q, r = quat[:, n.par, 0], quat[:, n.par, 2]
                sp.wait_ge(s["qkv_sb"], n.count(3, 3))
                done = s[f"rolled{n.par}"]
                sp.dma_start(r[HD:P], q[0:P - HD]).then_inc(done, 16)
                sp.dma_start(r[0:HD], q[P - HD:P]).then_inc(done, 16)

            roll(Turn(0, 0))
            roll(Turn(0, 1))

            def slot(m, more):
                n = Turn(m.base, m.k + 2)
                if n.k < B or more:
                    roll(n)
                if more and m.k == 1:
                    sp.wait_ge(s["wqkv_sb"], m.base + 1)
                    sp.dma_start(w_qkv_raw[:, :], qkv_w_dram[bass.ds(m.base + 1, 1)].rearrange("o p n -> p (o n)")).then_inc(s["wqkv_in"], 16)
                if more and m.k == B - 1:
                    sp.wait_ge(s["fc_ps"], m.base * (FK * B) + FK * B)
                    sp.dma_start(w_fc[:, :], fc_w_dram[bass.ds(m.base + 1, 1)].rearrange("o p n -> p (o n)")).then_inc(s["wfc_in"], 16)

            with sp.Fori(0, LAYERS - 1) as layer:
                for k in range(B):
                    slot(Turn(layer, k), True)
            for k in range(B):
                slot(Turn(LAYERS - 1, k), False)
            for b in range(B):
                sp.wait_ge(s["resulted"], b + 1)
                sp.dma_start(out_dram[b], result[:, b % 2]).then_inc(s[f"out{b % 2}_out"], 16)
            for par in range(2):
                sp.wait_ge(s[f"out{par}_out"], 32)

        @block.tensor
        def _(pe):
            def transposes(dst, src):
                for i in range(T):
                    last = pe.transpose(dst[:, i * P:(i + 1) * P], src[:, i], ident)
                return last

            pe.wait_ge(s["const_in"], 16)
            pe.wait_ge(s["par_in"], 11 * 16)
            pe.transpose(ps_spec[:, 0:LAYERS * NPAR], par_rows[:, :],
                         const[0:LAYERS * NPAR, C_ID:C_ID + LAYERS * NPAR]).then_inc(s["par_ps"], 1)
            pe.wait_ge(s["lin_in"], 32)
            pe.transpose(ps_out[0:2 * G, 0:P], lin_rows[:, :], ident).then_inc(s["linT_ps"], 1)
            for b in range(B):
                pe.wait_ge(s["x0_ready"], b + 1)
                if b:
                    pe.wait_ge(s["xt_sb"], b)
                transposes(ps_t, x_stream[:, T * b:T * b + T]).then_inc(s["xt_ps"], 1)
                pe.wait_ge(s["xt_sb"], b + 1)
                if b == 0:
                    pe.wait_ge(s["convw_made"], 1)
                if b >= 2:
                    pe.wait_ge(s["conv_sb"], b - 1)
                pe.matmul(ps_fc[0:2 * G, b % 2], w_conv[:, :], xT[:, b], start=True, stop=True).then_inc(s["conv_ps"], 1)

            def front(n):
                pe.wait_ge(s["ln1_norm"], n.count(1, 1))
                if isinstance(n.base, int) and n.base == 0 and n.k < 2:
                    pe.wait_ge(s["xt_sb"], B)
                if n.k:
                    pe.wait_ge(s["h1_sb"], n.count(1, 0))
                transposes(ps_t, normed[:, 0]).then_inc(s["t1_ps"], 1)
                pe.wait_ge(s["h1_sb"], n.count(1, 1))
                pe.wait_ge(s["wqkv_sb"], n.layer + 1)
                for j in range(3):
                    if n.k:
                        pe.wait_ge(s["qkv_sb"], n.count(3, j - 2))
                    pe.matmul(ps_qkv[:, j], w_qkv[:, j], h1[:, :], start=True, stop=True).then_inc(s["qkv_ps"], 1)

            front(Turn(0, 0))
            front(Turn(0, 1))

            pe.wait_ge(s["ffnw_in"], 32)
            pe.wait_ge(s["linT_sb"], 2)
            pe.wait_ge(s["linb_in"], 32)
            pe.wait_ge(s["gated"], 1)
            pe.wait_ge(s["gate_ones"], 1)
            pe.wait_ge(s["qkv_sb"], 6)

            def scores(i):
                b, c = i // T, (i % T) * P
                if i >= 2:
                    pe.wait_ge(s["logits_sb"], i - 1)
                    pe.wait_ge(s["branched"], i - 1)
                pe.matmul(ps_qkv[:, i % 2, 0:2 * E], gate[:, b, c:c + P], w_lin[:, :], start=True, stop=True).then_inc(s["logits_ps"], 1)
                pe.matmul(ps_fc[:, i % 2, 0:E], xT[:, b, c:c + P], w_ffn[:, :], start=True, stop=True).then_inc(s["full_ps"], 1)

            scores(0)
            for i in range(NT):
                if i + 1 < NT:
                    scores(i + 1)
                pe.wait_ge(s["sparsed"], i + 1)
                pe.wait_ge(s["sparse_sb"], i) if i else None
                pe.transpose(ps_t[:, 0:P], sparse[:, i % 2], ident).then_inc(s["sparse_ps"], 1)
                pe.wait_ge(s["sparse_sb"], i + 1)
                if i:
                    pe.wait_ge(s["acc_made"], i)
                pe.matmul(ps_out[:, 0:E], ones_row[:, :], ffn_bias[:, :], start=True, stop=False)
                pe.matmul(ps_out[:, 0:E], sparseT[:, i % 2], w_ffn[:, :], start=False, stop=True).then_inc(s["in_ps"], 1)

            pe.wait_ge(s["wproj_in"], 16)
            pe.matmul(ps_spec[:, :], hartley, w_proj[:, :], start=True, stop=True).then_inc(s["rproj_ps"], 1)
            pe.wait_ge(s["rproj_sb"], 1)
            pe.wait_ge(s["obias_in"], 32)
            pe.wait_ge(s["wmlp_in"], 16)
            pe.wait_ge(s["neg_made"], 1)
            pe.wait_ge(s["acc_made"], NT)

            def output(n, which, pieces, lhs):
                bias = out_bias[:, which, bass.ds(n.layer * E, E)]
                bias = bias.rearrange("p (o e) -> p o e", o=1).broadcast_to((P, T, E))
                pe.matmul(ps_out[:, :].rearrange("p (t e) -> p t e", t=T), ones_row[:, :], bias, start=True, stop=False,
                          skip_group_check=True)
                for i in range(T):
                    for k, w in enumerate(pieces):
                        last = pe.matmul(ps_out[:, i * E:(i + 1) * E], lhs(k, i), w, start=False,
                                         stop=(k == len(pieces) - 1), skip_group_check=True)
                return last

            def slot(m, more):
                pe.wait_ge(s["tripled"], m.count(1, 1))
                for j in range(4):
                    last = pe.matmul(ps_spec[:, :], neg_hartley[:, :] if j else hartley, triple[:, j],
                                     start=(j == 0), stop=(j == 3))
                last.then_inc(s["spec_ps"], 1)
                if m.k + 2 < B or more:
                    front(Turn(m.base, m.k + 2))
                pe.wait_ge(s["filter_sb"], m.count(1, 1))
                pe.wait_ge(s["x_ready"], m.count(1, B))
                output(m, 0, [w_rproj[:, bass.ds(m.layer * E, E)]],
                       lambda k, i: filtered[:, i * P:(i + 1) * P]).then_inc(s["attn_ps"], 1)
                pe.wait_ge(s["ln2_norm"], m.count(1, 1))
                pe.wait_ge(s["h1_sb"], m.count(1, 3) if (m.k + 2 < B or more) else LAYERS * B)
                transposes(ps_t, normed[:, 1]).then_inc(s["t2_ps"], 1)
                pe.wait_ge(s["h2_sb"], m.count(1, 1))
                pe.wait_ge(s["wfc_in"], m.layer * 16 + 16)
                for k in range(FK):
                    if k >= 2:
                        pe.wait_ge(s["gelued"], m.count(FK, k - 1))
                    pe.matmul(ps_fc[:, k % 2], w_fc[:, k * P:(k + 1) * P], h2[:, :], start=True, stop=True).then_inc(s["fc_ps"], 1)
                pe.wait_ge(s["gelued"], m.count(FK, FK))
                pe.wait_ge(s["x_mid"], m.count(1, 1))
                output(m, 1, [w_mlp[:, bass.ds(m.layer * (FK * E) + k * E, E)] for k in range(FK)],
                       lambda k, i: hidden[:, k, i * P:(i + 1) * P]).then_inc(s["mlp_ps"], 1)

            with pe.Fori(0, LAYERS - 1) as layer:
                for k in range(B):
                    slot(Turn(layer, k), True)
            for k in range(B):
                slot(Turn(LAYERS - 1, k), False)

        @block.scalar
        def _(act):
            act.wait_ge(s["par_ps"], 1)
            act.activation(par_all[:, :], ps_spec[:, 0:LAYERS * NPAR], ACT.Copy).then_inc(s["par_sb"], 1)
            act.wait_ge(s["gate_ones"], 1)
            act.wait_ge(s["linT_ps"], 1)
            for g in range(2):
                act.activation(w_lin[g * G:(g + 1) * G, g * E:(g + 1) * E], ps_out[g * G:(g + 1) * G, 0:P], ACT.Copy).then_inc(s["linT_sb"], 1)
            act.wait_ge(s["bott_in"], 6 * 16)
            for b in range(B):
                act.wait_ge(s["xt_ps"], b + 1)
                act.activation(xT[:, b], ps_t[:, :], ACT.Copy).then_inc(s["xt_sb"], 1)
                act.wait_ge(s["conv_ps"], b + 1)
                act.activation(conv_out[:, b], ps_fc[0:2 * G, b % 2], ACT.Identity, bias=bott[:, 0:1]).then_inc(s["conv_sb"], 1)

            def layer_vectors(dst, base, first, width, done):
                act.activation(dst[:, :], par_all[:, bass.ds(base * NPAR + first, width)], ACT.Copy).then_inc(done, 1)

            def front(n):
                if n.b == 0:
                    layer_vectors(par_pre, n.layer, 0, LN2W, s["par_pre_r"])
                    act.wait_ge(s["wqkv_in"], n.layer * 16 + 16)
                    if n.k:
                        act.wait_ge(s["qkv_ps"], n.count(3, 0))
                    act.activation(w_qkv[:, :].rearrange("p j (h d) -> p j h d", d=HD),
                                   w_qkv_raw[:, :].rearrange("p (h j d) -> p j h d", j=3, d=HD), ACT.Copy).then_inc(s["wqkv_sb"], 1)
                    act.wait_ge(s["par_pre_r"], n.layer + 1)
                act.wait_ge(s["t1_ps"], n.count(1, 1))
                if n.k:
                    act.wait_ge(s["qkv_ps"], n.count(3, 0))
                act.activation(h1[:, :], ps_t[:, :], ACT.Identity, bias=par_pre[:, LN1B:LN1B + 1],
                               scale=par_pre[:, LN1W:LN1W + 1]).then_inc(s["h1_sb"], 1)
                if n.k >= 2 or not isinstance(n.base, int):
                    act.wait_ge(s["tripled"], n.count(1, -1))
                    act.wait_ge(s["crossed"], n.count(1, -1))
                for j in range(3):
                    act.wait_ge(s["qkv_ps"], n.count(3, j + 1))
                    act.activation(quat[:, n.par, 0, j], ps_qkv[:, j], ACT.Identity,
                                   bias=par_pre[:, QKVB + j:QKVB + j + 1]).then_inc(s["qkv_sb"], 1)
                act.wait_ge(s["qkv_sb"], n.count(3, 3))
                if n.k:
                    act.wait_ge(s["fraced"], n.count(1, 0))
                    act.wait_ge(s["cosined"], n.count(1, 0))
                act.activation(turns[:, :], quat[:, n.par, 0], ACT.Identity, bias=0.25, scale=INV_TURN).then_inc(s["turned"], 1)
                act.wait_ge(s["turned"], n.count(1, 1))
                act.activation(frac[:, :], turns[:, :], ACT.Identity, bias=ROUND).then_inc(s["rounded"], 1)
                act.wait_ge(s["fraced"], n.count(1, 1))
                act.activation(quat[:, n.par, 3], frac[:, :], ACT.Sin, scale=-TURN).then_inc(s["cosined"], 1)

            act.wait_ge(s["par_sb"], 1)
            front(Turn(0, 0))
            front(Turn(0, 1))
            act.wait_ge(s["bn_shift"], 1)
            act.activation(gate[0:2 * G], conv_out[:, :], ACT.Gelu, bias=bn_sc[:, 3:4], scale=bn_sc[:, 1:2]).then_inc(s["gated"], 1)

            def logits_out(i):
                act.wait_ge(s["logits_ps"], i + 1)
                if i >= 2:
                    act.wait_ge(s["mr_r"], 8 * (i - 2) + 2)
                    act.wait_ge(s["exped"], 2 * (i - 1))
                act.activation(logits[:, i % 2], ps_qkv[:, i % 2, 0:2 * E], ACT.Copy).then_inc(s["logits_sb"], 1)

            logits_out(0)
            for i in range(NT):
                if i + 1 < NT:
                    logits_out(i + 1)
                act.wait_ge(s["negmax_r"], i + 1)
                act.wait_ge(s["logits_sb"], i + 1)
                if i >= 2:
                    act.wait_ge(s["kept_r"], 2 * (i - 1))
                    act.wait_ge(s["rsum_r"], i - 1)
                for g in range(2):
                    act.activation(expd[:, i % 2, g], logits[:, i % 2, g], ACT.Exp,
                                   bias=neg_max[:, i % 2, g:g + 1], accum_out=esum[:, i % 2, g:g + 1]).then_inc(s["exped"], 1)
                act.wait_ge(s["sparse_ps"], i + 1)
                if i >= 2:
                    act.wait_ge(s["in_ps"], i - 1)
                act.activation(sparseT[:, i % 2], ps_t[:, 0:P], ACT.Copy).then_inc(s["sparse_sb"], 1)
            act.wait_ge(s["rproj_ps"], 1)
            act.activation(w_rproj[:, :], ps_spec[:, :], ACT.Copy).then_inc(s["rproj_sb"], 1)

            def slot(m, more):
                if m.k + 2 < B or more:
                    front(Turn(m.base, m.k + 2))
                if m.b == 0:
                    layer_vectors(par_post, m.layer, LN2W, NPAR - LN2W, s["par_post_r"])
                    act.wait_ge(s["par_post_r"], m.layer + 1)
                act.wait_ge(s["t2_ps"], m.count(1, 1))
                act.activation(h2[:, :], ps_t[:, :], ACT.Identity, bias=par_post[:, LN2B - LN2W:LN2B - LN2W + 1],
                               scale=par_post[:, 0:1]).then_inc(s["h2_sb"], 1)
                if not (m.k + 2 < B or more):
                    act.wait_ge(s["mlp_ps"], m.count(1, 0))
                for k in range(FK):
                    act.wait_ge(s["fc_ps"], m.count(FK, k + 1))
                    f = FCB - LN2W + k
                    act.activation(hidden[:, k], ps_fc[:, k % 2], ACT.Gelu, bias=par_post[:, f:f + 1]).then_inc(s["gelued"], 1)

            with act.Fori(0, LAYERS - 1) as layer:
                for k in range(B):
                    slot(Turn(layer, k), True)
            for k in range(B):
                slot(Turn(LAYERS - 1, k), False)

        @block.vector
        def _(dve):
            tt, ts, stt = dve.tensor_tensor, dve.tensor_scalar, dve.scalar_tensor_tensor
            dve.memset(ones_row[:, :], 0.0)
            dve.memset(out_bias[:, :, :], 0.0)
            dve.memset(ffn_bias[:, :], 0.0).then_inc(s["zeroed"], 1)
            dve.wait_ge(s["zeroed"], 1)
            dve.memset(ones_row[0:1, :], 1.0)
            dve.memset(gate[2 * G:2 * G + 1, :, :], 1.0)
            dve.memset(quat[:, :, 1, :, 0:1], 0.0)
            dve.memset(dprod[:, 0:1], 0.0)
            dve.memset(w_lin[:, :], 0.0).then_inc(s["gate_ones"], 1)

            def layer_stats(n, which, raw, done, raw_count):
                stats = (stats1, stats2)[which][:, T * n.b:T * n.b + T]
                for i in range(T):
                    last = dve.bn_stats(stats[:, i], x_stream[:, T * n.b + i])
                last.then_inc(raw, 1)
                dve.wait_ge(raw, raw_count)
                dve.memset(pause[:, :], 0.0)
                for i in range(T):
                    last = dve.bn_aggr(meanvar[:, which, T * n.b + i], stats[:, i])
                last.then_inc(done, 1)

            def normalise(dst, src, b, mean, inverse):
                for i in range(T):
                    c = T * b + i
                    last = ts(dst[:, i], src[:, i], mean[:, c, 0:1], inverse[:, c:c + 1],
                              ALU.subtract, ALU.mult)
                return last

            for b in range(B):
                dve.wait_ge(s[f"x{b}_in"], 16)
                for i in range(T):
                    last = dve.bn_stats(stats0[:, T * b + i], x_in[:, T * b + i])
                last.then_inc(s["s0_raw"], 1)
                dve.wait_ge(s["s0_raw"], b + 1)
                for i in range(T):
                    last = dve.bn_aggr(meanvar0[:, T * b + i], stats0[:, T * b + i])
                last.then_inc(s["s0_mv"], 1)
            for b in range(B):
                dve.wait_ge(s["s0_rstd"], b + 1)
                normalise(x_stream[:, T * b:T * b + T], x_in[:, T * b:T * b + T], b, meanvar0, rstd0).then_inc(s["x0_ready"], 1)
            dve.wait_ge(s["conv_in"], 32)
            dve.wait_ge(s["const_in"], 16)
            for g in range(2):
                last = ts(w_conv[:, g * G:(g + 1) * G], group, conv_col[:, g:g + 1], None, ALU.mult)
            last.then_inc(s["convw_made"], 1)
            ts(neg_hartley[:, :], hartley, -1.0, None, ALU.mult).then_inc(s["neg_made"], 1)
            for b in range(B):
                dve.wait_ge(s["x0_ready"], b + 1)
                layer_stats(Turn(0, b), 0, s["ln1_raw"], s["ln1_stats"], b + 1)

            def front_norm(n):
                dve.wait_ge(s["ln1_rstd"], n.count(1, 1))
                if n.k:
                    dve.wait_ge(s["t1_ps"], n.count(1, 0))
                normalise(normed[:, 0], x_stream[:, n.tiles], n.b, meanvar[:, 0], rstd[:, 0]).then_inc(s["ln1_norm"], 1)

            def front_frac(n):
                dve.wait_ge(s["rounded"], n.count(1, 1))
                stt(frac[:, :], frac[:, :], ROUND, turns[:, :], ALU.subtract, ALU.subtract).then_inc(s["fraced"], 1)

            front_norm(Turn(0, 0))
            front_norm(Turn(0, 1))
            for b in range(B):
                dve.wait_ge(s["conv_sb"], b + 1)
                last = dve.bn_stats(bn_stats[:, b], conv_out[:, b])
            last.then_inc(s["bn_raw"], 1)
            dve.wait_ge(s["bn_raw"], 1)
            dve.bn_aggr(bn_mv[:, :], bn_stats[:, :]).then_inc(s["bn_mv_r"], 1)
            dve.wait_ge(s["bn_rstd"], 1)
            tt(bn_sc[:, 1:2], bott[:, 1:2], bn_sc[:, 0:1], ALU.mult).then_inc(s["bn_scale_r"], 1)
            dve.wait_ge(s["bn_scale_r"], 1)
            tt(bn_sc[:, 2:3], bn_mv[:, 0:1], bn_sc[:, 1:2], ALU.mult).then_inc(s["bn_ms_r"], 1)
            dve.wait_ge(s["bn_ms_r"], 1)
            tt(bn_sc[:, 3:4], bott[:, 2:3], bn_sc[:, 2:3], ALU.subtract).then_inc(s["bn_shift"], 1)
            front_frac(Turn(0, 0))
            front_frac(Turn(0, 1))

            m8 = [0]
            mr = [0]
            for i in range(NT):
                par = i % 2
                dve.wait_ge(s["logits_sb"], i + 1)
                for r in range(TOPK // 8):
                    for g in range(2):
                        src = left[:, par, g] if r else logits[:, par, g]
                        if r:
                            dve.wait_ge(s["mr_r"], 8 * i + 2 * (r - 1) + g + 1)
                        dve.max(top[:, par, g], src).then_inc(s["m8_r"], 1)
                    if r == 0:
                        dve.wait_ge(s["m8_r"], 8 * i + 2)
                        if i >= 2:
                            dve.wait_ge(s["exped"], 2 * (i - 1))
                        ts(neg_max[:, par, :], top[:, par, :, 0], -1.0, None, ALU.mult).then_inc(s["negmax_r"], 1)
                    for g in range(2):
                        src = left[:, par, g] if r else logits[:, par, g]
                        dve.wait_ge(s["m8_r"], 8 * i + 2 * r + g + 1)
                        dve.match_replace(left[:, par, g], top[:, par, g], src, SELECTED).then_inc(s["mr_r"], 1)
                dve.wait_ge(s["exped"], 2 * i + 2)
                dve.reciprocal(rsum[:, par, :], esum[:, par, :]).then_inc(s["rsum_r"], 1)
                for g in range(2):
                    dve.wait_ge(s["mr_r"], 8 * i + 7 + g)
                    stt(kept[:, par, g], left[:, par, g], SELECTED, expd[:, par, g], ALU.is_equal, ALU.mult).then_inc(s["kept_r"], 1)
                dve.wait_ge(s["rsum_r"], i + 1)
                dve.wait_ge(s["kept_r"], 2 * i + 1)
                dve.wait_ge(s["full_ps"], i + 1)
                if i >= 2:
                    dve.wait_ge(s["branch_xed"], i - 1)
                    dve.wait_ge(s["sparse_ps"], i - 1)
                stt(branch[:, par], kept[:, par, 0], rsum[:, par, 0:1], ps_fc[:, par, 0:E], ALU.mult, ALU.mult).then_inc(s["branched"], 1)
                dve.wait_ge(s["kept_r"], 2 * i + 2)
                stt(sparse[:, par], kept[:, par, 1], rsum[:, par, 1:2], x_stream[:, i], ALU.mult, ALU.mult).then_inc(s["sparsed"], 1)
                if i:
                    dve.wait_ge(s["in_ps"], i)
                    dve.wait_ge(s["branch_xed"], i)
                    tt(acc[:, i - 1], ps_out[:, 0:E], branch_x[:, 1 - par], ALU.add).then_inc(s["acc_made"], 1)
            dve.wait_ge(s["in_ps"], NT)
            dve.wait_ge(s["branch_xed"], NT)
            tt(acc[:, NT - 1], ps_out[:, 0:E], branch_x[:, (NT - 1) % 2], ALU.add).then_inc(s["acc_made"], 1)

            def comps(n, j):
                return quat[:, n.par, :, j]

            def products_1(n):
                a, b = comps(n, 0), comps(n, 1)
                dve.wait_ge(s["diffed"], n.count(1, 1))
                dve.wait_ge(s["cosined"], n.count(1, 1))
                dve.wait_ge(s[f"rolled{n.par}"], n.pairs(32, 32))
                tt(square[:, :], a, b, ALU.mult).then_inc(s["squared"], 1)
                tt(prod_a[:, :], a[:, 0:1].broadcast_to((P, 2, S)), b[:, 2:4], ALU.mult).then_inc(s["pa_r"], 1)
                tt(prod_b[:, :], a[:, 2:4], b[:, 0:1].broadcast_to((P, 2, S)), ALU.mult).then_inc(s["pb_r"], 1)

            def products_2(n):
                a, b = comps(n, 0), comps(n, 1)
                one = n.count(1, 1)
                dve.wait_ge(s["squared"], one)
                tt(dprod[:, 1:S], square[:, 0, 1:S], square[:, 0, 0:S - 1], ALU.subtract).then_inc(s["d_r"], 1)
                tt(prod_c[:, 0], square[:, 0], square[:, 1], ALU.subtract)
                tt(prod_c[:, 1], square[:, 2], square[:, 3], ALU.add).then_inc(s["u_r"], 1)
                dve.wait_ge(s["d_r"], one)
                tt(four_p[:, 1], dprod[:, :], square[:, 1], ALU.add).then_inc(s["c1a_r"], 1)
                dve.wait_ge(s["u_r"], one)
                tt(four_p[:, 0], prod_c[:, 0], prod_c[:, 1], ALU.subtract).then_inc(s["c0_r"], 1)
                dve.wait_ge(s["pb_r"], one)
                tt(prod_a[:, :], prod_a[:, :], prod_b[:, :], ALU.add).then_inc(s["pc_r"], 1)

            def products_3(n):
                a, b = comps(n, 0), comps(n, 1)
                one = n.count(1, 1)
                dve.wait_ge(s["c0_r"], one)
                tt(prod_c[:, 0], a[:, 2], b[:, 3], ALU.mult)
                tt(prod_c[:, 1], a[:, 3], b[:, 2], ALU.mult).then_inc(s["zy_r"], 1)
                dve.wait_ge(s["crossed"], one)
                dve.wait_ge(s["pc_r"], one)
                tt(four_p[:, 2], prod_a[:, 0], cross_b[:, 1], ALU.add)
                tt(four_p[:, 3], prod_a[:, 1], cross_b[:, 0], ALU.subtract).then_inc(s["c23_r"], 1)
                dve.wait_ge(s["zy_r"], one)
                tt(prod_c[:, 0], prod_c[:, 0], prod_c[:, 1], ALU.subtract).then_inc(s["zz_r"], 1)
                dve.wait_ge(s["zz_r"], one)
                dve.wait_ge(s["c1a_r"], one)
                tt(four_p[:, 1], four_p[:, 1], prod_c[:, 0], ALU.add).then_inc(s["c1_r"], 1)

            def products_4(n):
                dve.wait_ge(s["c1_r"], n.count(1, 1))
                dve.wait_ge(s["c23_r"], n.count(1, 1))
                if n.k:
                    dve.wait_ge(s["spec_ps"], n.count(1, 0))
                tt(triple[:, :], four_p[:, :], comps(n, 2), ALU.mult).then_inc(s["tripled"], 1)

            products_1(Turn(0, 0))
            products_2(Turn(0, 0))
            products_3(Turn(0, 0))
            products_4(Turn(0, 0))

            def tiles3(ap):
                return ap.rearrange("p (t e) -> p t e", t=T)

            def slot(m, more):
                has_next = m.k + 1 < B or more
                has_front = m.k + 2 < B or more
                n = Turn(m.base, m.k + 1)
                f = Turn(m.base, m.k + 2)
                if has_front:
                    front_norm(f)
                if has_next:
                    products_1(n)
                dve.wait_ge(s["spec_ps"], m.count(1, 1))
                tt(filtered[:, :], ps_spec[:, :], gain, ALU.mult).then_inc(s["filter_sb"], 1)
                if has_next:
                    products_2(n)
                dve.wait_ge(s["attn_ps"], m.count(1, 1))
                x = x_stream[:, m.tiles]
                tt(x, tiles3(ps_out[:, :]), x, ALU.add).then_inc(s["x_mid"], 1)
                dve.wait_ge(s["x_mid"], m.count(1, 1))
                layer_stats(m, 1, s["ln2_raw"], s["ln2_stats"], m.count(1, 1))
                if has_front:
                    front_frac(f)
                dve.wait_ge(s["ln2_rstd"], m.count(1, 1))
                normalise(normed[:, 1], x, m.b, meanvar[:, 1], rstd[:, 1]).then_inc(s["ln2_norm"], 1)
                if has_next:
                    products_3(n)
                    products_4(n)
                dve.wait_ge(s["mlp_ps"], m.count(1, 1))
                if more:
                    tt(x, tiles3(ps_out[:, :]), x, ALU.add).then_inc(s["x_ready"], 1)
                    dve.wait_ge(s["x_ready"], m.count(1, 1 + B))
                    layer_stats(m, 0, s["ln1_raw"], s["ln1_stats"], m.count(1, 1 + B))
                else:
                    dve.wait_ge(s["acc_mid"], m.b + 1)
                    if m.b >= 2:
                        dve.wait_ge(s[f"out{m.b % 2}_out"], 16)
                    tt(result[:, m.b % 2], tiles3(ps_out[:, :]), acc[:, m.tiles], ALU.add).then_inc(s["resulted"], 1)
                    if m.b < B - 1:
                        dve.sem_inc(s["x_ready"], 1)

            for _ in range(B):
                dve.sem_inc(s["x_ready"], 1)
            with dve.Fori(0, LAYERS - 1) as layer:
                for k in range(B):
                    slot(Turn(layer, k), True)
            for k in range(B):
                slot(Turn(LAYERS - 1, k), False)

        @block.gpsimd
        def _(pool):
            tt, ts = pool.tensor_tensor, pool.tensor_scalar
            pool.memset(eps_tile[:, :], EPS)
            pool.memset(minus_half[:, :], -0.5).then_inc(s["const_made"], 1)
            pool.wait_ge(s["const_made"], 1)

            def inverse_std(b, mv, ve, rs, ready, ready_count, eps_done, eps_count, done):
                c = slice(T * b, T * b + T)
                pool.wait_ge(ready, ready_count)
                tt(ve[:, c], mv[:, c, 1], eps_tile[:, :], ALU.add).then_inc(eps_done, 1)
                pool.wait_ge(eps_done, eps_count)
                tt(rs[:, c], ve[:, c], minus_half[:, c], ALU.pow).then_inc(done, 1)

            def rstd_front(n):
                inverse_std(n.b, meanvar[:, 0], var_eps[:, 0], rstd[:, 0], s["ln1_stats"], n.count(1, 1), s["ln1_eps"], n.count(1, 1), s["ln1_rstd"])

            def rstd_back(n):
                inverse_std(n.b, meanvar[:, 1], var_eps[:, 1], rstd[:, 1], s["ln2_stats"], n.count(1, 1), s["ln2_eps"], n.count(1, 1), s["ln2_rstd"])

            for b in range(B):
                inverse_std(b, meanvar0, var_eps0, rstd0, s["s0_mv"], b + 1, s["s0_eps"], b + 1, s["s0_rstd"])
            for b in range(B):
                rstd_front(Turn(0, b))

            def diff(n):
                x, d = quat[:, n.par, 0], quat[:, n.par, 1]
                pool.wait_ge(s["qkv_sb"], n.count(3, 3))
                tt(d[:, :, 1:S], x[:, :, 1:S], x[:, :, 0:S - 1], ALU.subtract).then_inc(s["diffed"], 1)

            pool.wait_ge(s["bn_mv_r"], 1)
            ts(bn_sc[:, 2:3], bn_mv[:, 1:2], EPS, 1.0, ALU.add, ALU.mult).then_inc(s["bn_eps_r"], 1)
            pool.wait_ge(s["bn_eps_r"], 1)
            tt(bn_sc[:, 0:1], bn_sc[:, 2:3], minus_half[0:2 * G, 0:1], ALU.pow).then_inc(s["bn_rstd"], 1)
            diff(Turn(0, 0))
            diff(Turn(0, 1))
            for i in range(NT):
                pool.wait_ge(s["branched"], i + 1)
                if i >= 2:
                    pool.wait_ge(s["acc_made"], i - 1)
                tt(branch_x[:, i % 2], branch[:, i % 2], x_in[:, i], ALU.add).then_inc(s["branch_xed"], 1)

            def cross(n):
                a, b = quat[:, n.par, :, 0], quat[:, n.par, :, 1]
                pool.wait_ge(s["diffed"], n.count(1, 1))
                pool.wait_ge(s["cosined"], n.count(1, 1))
                pool.wait_ge(s[f"rolled{n.par}"], n.pairs(32, 32))
                if n.k:
                    pool.wait_ge(s["c23_r"], n.count(1, 0))
                tt(cross_a[:, :], a[:, 1:2].broadcast_to((P, 2, S)), b[:, 2:4], ALU.mult)
                tt(cross_b[:, :], a[:, 2:4], b[:, 1:2].broadcast_to((P, 2, S)), ALU.mult).then_inc(s["crossa_r"], 1)
                pool.wait_ge(s["crossa_r"], n.count(1, 1))
                tt(cross_b[:, :], cross_b[:, :], cross_a[:, :], ALU.subtract).then_inc(s["crossed"], 1)

            cross(Turn(0, 0))

            def slot(m, more):
                if m.k + 1 < B or more:
                    cross(Turn(m.base, m.k + 1))
                rstd_back(m)
                if m.k + 2 < B or more:
                    diff(Turn(m.base, m.k + 2))
                if more:
                    rstd_front(Turn(m.base, m.k + B))
                else:
                    pool.wait_ge(s["x_mid"], m.count(1, 1))
                    tt(acc[:, m.tiles], acc[:, m.tiles], x_stream[:, m.tiles], ALU.add).then_inc(s["acc_mid"], 1)

            with pool.Fori(0, LAYERS - 1) as layer:
                for k in range(B):
                    slot(Turn(layer, k), True)
            for k in range(B):
                slot(Turn(LAYERS - 1, k), False)


_INS = (["L0_attn_" + n for n in ("x", "ln1_w", "ln1_b", "attn_w", "attn_b", "aproj_w", "aproj_b", "ln2_w", "ln2_b",
                                  "fc_w", "fc_b", "mproj_w", "mproj_b")]
        + ["L0_ffn_weight", "L0_ffn_bias"]
        + [f"L0_ffn_{g}_{n}" for g in ("so", "si") for n in ("conv_w", "conv_b", "gamma", "beta", "lin_w", "lin_b")])


def kernel(**inputs):
    import numpy as _np
    import concourse.bacc as _bacc
    from concourse import mybir as _mybir
    from concourse.bass_utils import run_bass_kernel_spmd as _run

    nc = _bacc.Bacc("TRN2", target_bir_lowering=False, num_devices=1)
    arrays, aps = {}, {}
    for name in _INS:
        a = _np.ascontiguousarray(inputs[name])
        arrays[f"in_{name}_dram"] = a
        aps[name] = nc.dram_tensor(f"in_{name}_dram", a.shape, _mybir.dt.from_np(a.dtype), kind="ExternalInput").ap()
    c = shape_constants()
    arrays["shape_constants_dram"] = c
    consts = nc.dram_tensor("shape_constants_dram", c.shape, _mybir.dt.float32, kind="ExternalInput").ap()
    out = nc.dram_tensor("out_0_dram", (B, S, E), _mybir.dt.float32, kind="ExternalOutput").ap()
    build(nc, aps, consts, out)
    r = _run(nc, [arrays], core_ids=[0])
    return r.results[0]["out_0_dram"]
```

```python
from contextlib import ExitStack

import numpy as np

import concourse.bass as bass
from concourse import mybir

F32 = mybir.dt.float32
BF16 = mybir.dt.bfloat16
ALU = mybir.AluOpType
ACT = mybir.ActivationFunctionType

P = 128
B, S, E = 4, 512, 128
H, HD = 16, 8
LAYERS = 4
T = S // P
NT = B * T
FF = 4 * E
FK = FF // P
G = E // 4
TOPK = 32
EPS = 1e-5
TURN = 6.283185
INV_TURN = 1.0 / (2.0 * np.pi)
ROUND = 12582912.0
SELECTED = -3.0e38
NPAR = 11
LN1W, LN1B, QKVB, LN2W, LN2B, FCB = 0, 1, 2, 5, 6, 7
C_R, C_ID, C_GAIN, C_GROUP = 0, 128, 256, 768
NCONST = C_GROUP + G
NBIAS = 2 * LAYERS * E + E
PART_ROWS = (0, 64, 96)


def shape_constants():
    def cas(n):
        a = 2.0 * np.pi * np.outer(np.arange(n), np.arange(n)) / n
        return np.cos(a) + np.sin(a)
    c = np.zeros((P, NCONST), np.float64)
    c[:, C_R:C_R + E] = np.kron(cas(H), cas(HD)) / np.sqrt(E)
    c[:, C_ID:C_ID + P] = np.eye(P)
    kh = np.fft.fftfreq(H)[:, None, None]
    kd = np.fft.fftfreq(HD)[None, :, None]
    ks = np.fft.fftfreq(S)[None, None, :]
    km = np.sqrt(ks ** 2 + kh ** 2 + kd ** 2 + 1e-10)
    gain = np.cos(np.arctan(np.log(km + 1e-10))).reshape(E, S)
    lam = np.arange(S) / S
    t = np.arange(S) * 0.1
    mod = np.sin(t + lam) * np.cos(t - 2.0 * lam + 0.5 * lam ** 2)
    c[:, C_GAIN:C_GAIN + S] = gain * (1.0 + 0.1 * mod)
    c[:, C_GROUP:C_GROUP + G] = (np.arange(P)[:, None] // 4 == np.arange(G)[None, :])
    return c.astype(np.float32)


class Turn:

    def __init__(self, layer, k):
        self.base, self.k = layer, k
        self.static = isinstance(layer, int)
        self.layer = layer + k // B if k // B else layer
        self.b = k % B
        self.par = k % 2
        self.tiles = slice(T * self.b, T * self.b + T)

    def plus(self, d):
        return Turn(self.base, self.k + d)

    def exists(self):
        return not self.static or 0 <= self.k < NT // T * LAYERS

    def through(self, ago=0):
        return self.count(1, 1 - ago)

    def count(self, per=1, plus=0):
        assert self.static or self.k * per + plus > 0
        return self.base * (B * per) + (self.k * per + plus)

    def pairs(self, per, plus=0):
        assert self.static or self.k // 2 * per + plus > 0
        return self.base * (B // 2 * per) + (self.k // 2 * per + plus)


FILLS = [("t2", 1), ("fc1", 1), ("t1", 4), ("fc0", 1), ("q", 4), ("v", 4), ("k", 4), ("st", 1), ("qd", 4),
         ("fc2", 1), ("fc3", 1), ("vd", 4), ("kd", 4), ("lg", 3)]
OUTS = [("proj", 2), ("ffn1", 1), ("mlp", 1)]
OUT_READ = {"proj": "x_mid", "ffn1": "acc_made", "mlp": "x_ready"}
AHEAD = 4

FILL_COUNT = len(FILLS)
assert FILL_COUNT % 2 == 0
SLOTS = B * LAYERS


def step_before(order, stride, name, n):
    names = [x for x, _ in order]
    at = names.index(name)
    slot = n.plus(-order[at][1])
    for _ in range(SLOTS * len(order)):
        at -= stride
        if at < 0:
            at += len(order)
            slot = slot.plus(-1)
        other = slot.plus(order[at][1])
        if other.exists():
            return names[at], other
    return None


def build(nc, t, consts, out):
    with ExitStack() as ctx:
        def sb(name, shape, dt=F32):
            return ctx.enter_context(nc.sbuf_tensor(name, shape, dt))

        def psum(name, shape):
            return ctx.enter_context(nc.psum_tensor(name, shape, F32))

        def sem(name):
            return ctx.enter_context(nc.semaphore(name))

        const = sb("const", [P, NCONST])
        hartley = const[:, C_R:C_R + E]
        ident = const[:, C_ID:C_ID + P]
        gain = const[:, C_GAIN:C_GAIN + S]
        group = const[:, C_GROUP:C_GROUP + G]
        neg_hartley = sb("neg_hartley", [P, E])
        pause = sb("pause", [P, 64])
        eps_tile = sb("eps_tile", [P, T])
        zeros = sb("zeros", [P, T])
        minus_half = sb("minus_half", [P, NT])
        x_in = sb("x_in", [P, NT, E])
        x_flat = x_in[:, :, :].rearrange("p t e -> p (t e)")
        x_stream = sb("x_stream", [P, NT, E])
        par_rows = sb("par_rows", [LAYERS * NPAR, P])
        par_all = sb("par_all", [P, LAYERS * NPAR])
        par_ln1 = sb("par_ln1", [P, 2])
        par_qkv = sb("par_qkv", [P, 3])
        par_ln2 = sb("par_ln2", [P, 2])
        par_fc = sb("par_fc", [P, FK])
        bias_rows = sb("bias_rows", [P, NBIAS])
        bias_rest = sb("bias_rest", [P, NBIAS])
        bias_parts = sb("bias_parts", [P, NBIAS], BF16)
        ones_3 = sb("ones_3", [P, P], BF16)
        w_qkv_raw = sb("w_qkv_raw", [P, LAYERS * 3 * E])
        w_qkv = sb("w_qkv", [P, 3, E])
        w_fc = sb("w_fc", [P, FF])
        w_mlp = sb("w_mlp", [P, LAYERS * FK * E])
        w_proj = sb("w_proj", [P, LAYERS * E])
        w_rproj = sb("w_rproj", [P, LAYERS * E])
        stats = [sb(f"stats{i}", [P, NT, 6]) for i in range(3)]
        meanvar = [sb(f"meanvar{i}", [P, NT, 2]) for i in range(3)]
        var_eps = [sb(f"var_eps{i}", [P, NT]) for i in range(3)]
        rstd = [sb(f"rstd{i}", [P, NT]) for i in range(3)]
        mean_rstd = [sb(f"mean_rstd{i}", [P, NT]) for i in range(3)]
        shift = [sb(f"shift{i}", [P, NT]) for i in range(3)]
        normed = sb("normed", [P, 2, T, E])
        h1 = sb("h1", [P, S])
        h2 = sb("h2", [P, S])
        h_diff = sb("h_diff", [P, S])
        quat = sb("quat", [P, 2, 4, 3, S])
        turns = sb("turns", [P, 3, S])
        frac = sb("frac", [P, 3, S])
        square01 = sb("square01", [P, 2, S])
        square23 = sb("square23", [P, 2, S])
        sum23 = sb("sum23", [P, S])
        prod_20 = sb("prod_20", [P, 2, S])
        prod_23 = sb("prod_23", [P, 2, S])
        cross_a = sb("cross_a", [P, 2, S])
        cross_b = sb("cross_b", [P, 2, S])
        cross = sb("cross", [P, 2, S])
        triple = sb("triple", [P, 4, S])
        filtered = sb("filtered", [P, S])
        hidden = sb("hidden", [P, FK, S])
        result = sb("result", [P, 2, T, E])
        conv_col = sb("conv_col", [P, 2])
        w_conv = sb("w_conv", [P, 2 * G])
        bott = sb("bott", [2 * G, 4])
        conv_out = sb("conv_out", [2 * G, B * S])
        gate = sb("gate", [2 * G + 1, 2, P])
        lin_rows = sb("lin_rows", [P, 2 * G])
        w_lin = sb("w_lin", [2 * G + 1, 2 * E])
        w_ffn = sb("w_ffn", [P, E])
        bn_stats = sb("bn_stats", [2 * G, B, 6])
        bn_mv = sb("bn_mv", [2 * G, 2])
        bn_sc = sb("bn_sc", [2 * G, 4])
        x_hat = sb("x_hat", [P, 2, E])
        x_hatT = sb("x_hatT", [P, 2, P])
        logits = sb("logits", [P, 2, 2, E])
        left = sb("left", [P, 2, 2, E])
        top = sb("top", [P, 2, 2, 8])
        neg_max = sb("neg_max", [P, 2, 2])
        expd = sb("expd", [P, 2, 2, E])
        esum = sb("esum", [P, 2, 2])
        rsum = sb("rsum", [P, 2, 2])
        kept = sb("kept", [P, 2, 2, E])
        branch = sb("branch", [P, 2, E])
        branch_x = sb("branch_x", [P, 2, E])
        sparse = sb("sparse", [P, 2, E])
        sparseT = sb("sparseT", [P, 2, P])

        ps_rot = psum("ps_rot", [P, 2, S])
        ps_spec = psum("ps_spec", [P, S])
        ps_out = psum("ps_out", [P, S])
        ps_c = psum("ps_c", [P, 4, S])

        s = {name: sem(name) for name in (
            "x0_in x1_in x2_in x3_in const_in par_in wproj_in wqkv_in wfc_in wmlp_in bias_in conv_in lin_in "
            "bott_in ffnw_in linb_in out0_out out1_out rolled0 rolled1 "
            "const_made zeroed neg_made convw_made w_lin_zero bias_hi bias_rem bias_mid bias_rem2 bias_lo "
            "start_ps start_sb s0_raw s0_mv s0_eps s0_rstd x0_ready bn_raw bn_mv_r bn_eps_r bn_rstd "
            "bn_scale_r bn_ms_r bn_shift gated hatted negmax_r exped topped0 topped1 topped2 topped3 struck0 struck1 struck2 struck3 rsum_r kept_r sparsed "
            "ffn_ps branched branch_xed acc_made "
            "ln1_raw ln1_stats ln1_eps ln1_rstd ln1_mr ln1_shift ln1_norm "
            "ln2_raw ln2_stats ln2_eps ln2_rstd ln2_mr ln2_shift ln2_norm "
            "diffed turned rounded fraced cosined par_ln1_r par_qkv_r par_ln2_r par_fc_r wqkv_sb xhat_sb "
            "sq01_r sq23_raw sq23_r p20_r p23_r crossa_r crossb_r crossed c23a_r c0a_r c1z_r c1a_r c1b_r c1c_r c23b_r "
            "c0_made c1_made c23_made tripled spec_ps filter_sb attn_ps x_mid mlp_ps x_ready resulted"
        ).split()}
        s.update({name + end: sem(name + end) for name, _ in FILLS for end in ("_ps", "_sb")})

        x_dram = t["L0_attn_x"].rearrange("b s e -> (b s) e").rearrange("(b t p) e -> b p t e", t=T, p=P)
        out_dram = out.rearrange("b s e -> (b s) e").rearrange("(b t p) e -> b p t e", t=T, p=P)
        fc_w_dram = t["L0_attn_fc_w"]

        def run_slots(engine, slot):
            def write(u):
                def at(lag, step, *args):
                    if u.plus(lag).exists():
                        step(u.plus(lag), *args)
                slot(at)
            for k in range(-AHEAD, 0):
                write(Turn(0, k))
            with engine.Fori(0, LAYERS - 1) as layer:
                for k in range(B):
                    write(Turn(layer, k))
            for k in range(SLOTS - B, SLOTS):
                write(Turn(0, k))

        block = ctx.enter_context(nc.Block())

        @block.sync
        def _(sp):
            for b in range(B):
                sp.dma_start(x_in[:, T * b:T * b + T, :], x_dram[b]).then_inc(s[f"x{b}_in"], 16)
                if b == 0:
                    sp.dma_start(const[:, :], consts).then_inc(s["const_in"], 16)
            for g, name in enumerate(("so", "si")):
                sp.dma_start(conv_col[:, g:g + 1],
                             t[f"L0_ffn_{name}_conv_w"].rearrange("g (f o) -> (g f) o", o=1)).then_inc(s["conv_in"], 16)
            for row, name in ((LN1W, "ln1_w"), (LN1B, "ln1_b"), (LN2W, "ln2_w"), (LN2B, "ln2_b")):
                sp.dma_start(par_rows[row:row + NPAR * (LAYERS - 1) + 1:NPAR, :],
                             t["L0_attn_" + name]).then_inc(s["par_in"], 16)
            for j in range(3):
                sp.dma_start(
                    par_rows[QKVB + j:QKVB + j + NPAR * (LAYERS - 1) + 1:NPAR, :].rearrange("l (h d) -> l h d", d=HD),
                    t["L0_attn_attn_b"].rearrange("l (h j d) -> j l h d", j=3, d=HD)[j]).then_inc(s["par_in"], 16)
            for k in range(FK):
                sp.dma_start(par_rows[FCB + k:FCB + k + NPAR * (LAYERS - 1) + 1:NPAR, :],
                             t["L0_attn_fc_b"][:, k * P:(k + 1) * P]).then_inc(s["par_in"], 16)
            for g, name in enumerate(("so", "si")):
                sp.dma_start(lin_rows[:, g * G:(g + 1) * G], t[f"L0_ffn_{name}_lin_w"]).then_inc(s["lin_in"], 16)
                for c, vec in enumerate(("conv_b", "gamma", "beta")):
                    sp.dma_start(bott[g * G:(g + 1) * G, c:c + 1],
                                 t[f"L0_ffn_{name}_{vec}"].rearrange("(g o) -> g o", o=1)).then_inc(s["bott_in"], 16)
            sp.dma_start(w_qkv_raw[:, :].rearrange("p (l n) -> p l n", l=LAYERS),
                         t["L0_attn_attn_w"].rearrange("l p n -> p l n")).then_inc(s["wqkv_in"], 16)
            sp.dma_start(w_proj[:, :].rearrange("p (l e) -> p l e", l=LAYERS),
                         t["L0_attn_aproj_w"].rearrange("l i e -> i l e")).then_inc(s["wproj_in"], 16)
            sp.dma_start(w_ffn[:, :], t["L0_ffn_weight"]).then_inc(s["ffnw_in"], 16)
            sp.wait_ge(s["w_lin_zero"], 1)
            for g, name in enumerate(("so", "si")):
                sp.dma_start(w_lin[2 * G:2 * G + 1, g * E:(g + 1) * E],
                             t[f"L0_ffn_{name}_lin_b"].rearrange("(o e) -> o e", o=1)).then_inc(s["linb_in"], 16)
            sp.wait_ge(s["zeroed"], 1)
            for row in PART_ROWS:
                for w, name in enumerate(("aproj", "mproj")):
                    sp.dma_start(bias_rows[row:row + 1, w * LAYERS * E:(w + 1) * LAYERS * E],
                                 t[f"L0_attn_{name}_b"].rearrange("(o l) e -> o (l e)", o=1)).then_inc(s["bias_in"], 16)
                sp.dma_start(bias_rows[row:row + 1, 2 * LAYERS * E:NBIAS],
                             t["L0_ffn_bias"].rearrange("(o e) -> o e", o=1)).then_inc(s["bias_in"], 16)
            sp.dma_start(w_fc[:, :], fc_w_dram[0]).then_inc(s["wfc_in"], 16)
            sp.dma_start(w_mlp[:, :].rearrange("p (l k e) -> p l k e", l=LAYERS, k=FK),
                         t["L0_attn_mproj_w"].rearrange("l (k p) e -> p l k e", p=P)).then_inc(s["wmlp_in"], 16)

            def roll(n):
                q, r = quat[:, n.par, 0], quat[:, n.par, 2]
                for j in "qkv":
                    sp.wait_ge(s[j + "_sb"], n.through())
                done = s[f"rolled{n.par}"]
                sp.dma_start(r[HD:P], q[0:P - HD]).then_inc(done, 16)
                sp.dma_start(r[0:HD], q[P - HD:P]).then_inc(done, 16)

            def next_fc(n):
                if n.b == B - 1 and not (n.static and n.layer == LAYERS - 1):
                    for k in range(FK):
                        sp.wait_ge(s[f"fc{k}_ps"], n.through())
                    sp.dma_start(w_fc[:, :], fc_w_dram[bass.ds(n.layer + 1, 1)].rearrange("o p n -> p (o n)")).then_inc(s["wfc_in"], 16)

            def slot(at):
                at(4, roll)
                at(2, next_fc)

            run_slots(sp, slot)
            for b in range(B):
                sp.wait_ge(s["resulted"], b + 1)
                sp.dma_start(out_dram[b], result[:, b % 2]).then_inc(s[f"out{b % 2}_out"], 16)
            for par in range(2):
                sp.wait_ge(s[f"out{par}_out"], 32)

        @block.tensor
        def _(pe):
            def bank(name, n):
                before = step_before(FILLS, 2, name, n)
                if before:
                    pe.wait_ge(s[before[0] + "_sb"], before[1].through())
                return ps_rot[:, [x for x, _ in FILLS].index(name) % 2]

            def out_free(name, n):
                before = step_before(OUTS, 1, name, n)
                if before:
                    pe.wait_ge(s[OUT_READ[before[0]]], before[1].through())

            def transposes(dst, src):
                for i in range(T):
                    last = pe.transpose(dst[:, i * P:(i + 1) * P], src[:, i], ident)
                return last

            starts = 0

            def start_bank():
                nonlocal starts
                if starts >= 2:
                    pe.wait_ge(s["start_sb"], starts - 1)
                starts += 1
                return ps_rot[:, (starts - 1) % 2]

            pe.wait_ge(s["const_in"], 16)
            pe.wait_ge(s["par_in"], 11 * 16)
            pe.transpose(start_bank()[:, 0:LAYERS * NPAR], par_rows[:, :],
                         const[0:LAYERS * NPAR, C_ID:C_ID + LAYERS * NPAR]).then_inc(s["start_ps"], 1)
            pe.wait_ge(s["lin_in"], 32)
            pe.transpose(start_bank()[0:2 * G, 0:P], lin_rows[:, :], ident).then_inc(s["start_ps"], 1)
            for b in range(B):
                pe.wait_ge(s["x0_ready"], b + 1)
                transposes(start_bank(), x_stream[:, T * b:T * b + T]).then_inc(s["start_ps"], 1)
                pe.wait_ge(s["start_sb"], starts)
                pe.wait_ge(s["convw_made"], 1)
                pe.matmul(start_bank()[0:2 * G], w_conv[:, :], (h1, h2)[b % 2][:, :], start=True, stop=True).then_inc(s["start_ps"], 1)
            pe.wait_ge(s["wproj_in"], 16)
            pe.matmul(start_bank(), hartley, w_proj[:, :], start=True, stop=True).then_inc(s["start_ps"], 1)

            pe.wait_ge(s["start_sb"], starts)
            def t1(n):
                pe.wait_ge(s["ln1_norm"], n.through())
                transposes(bank("t1", n), normed[:, 0]).then_inc(s["t1_ps"], 1)

            def qkv(n, j):
                name = "qkv"[j]
                pe.wait_ge(s["t1_sb"], n.through())
                pe.wait_ge(s["wqkv_sb"], n.layer + 1)
                pe.matmul(bank(name, n), w_qkv[:, j], h1[:, :], start=True, stop=True).then_inc(s[name + "_ps"], 1)

            def qkv_diff(n, j):
                name = "qkv"[j] + "d"
                pe.wait_ge(s["diffed"], n.through())
                pe.wait_ge(s["wqkv_sb"], n.layer + 1)
                pe.matmul(bank(name, n), w_qkv[:, j], h_diff[:, :], start=True, stop=True).then_inc(s[name + "_ps"], 1)

            def t2(n):
                pe.wait_ge(s["ln2_norm"], n.through())
                transposes(bank("t2", n), normed[:, 1]).then_inc(s["t2_ps"], 1)

            def fc(n, k):
                name = f"fc{k}"
                pe.wait_ge(s["t2_sb"], n.through())
                pe.wait_ge(s["wfc_in"], n.layer * 16 + 16)
                pe.matmul(bank(name, n), w_fc[:, k * P:(k + 1) * P], h2[:, :], start=True, stop=True).then_inc(s[name + "_ps"], 1)

            def scores(i):
                room = bank("lg", i)
                pe.wait_ge(s["hatted"], i.through())
                pe.transpose(room[:, 2 * E:2 * E + P], x_hat[:, i.par], ident)
                pe.wait_ge(s["gated"], i.through())
                pe.matmul(room[:, 0:2 * E], gate[:, i.par], w_lin[:, :], start=True, stop=True).then_inc(s["lg_ps"], 1)

            def sparse_t(i):
                pe.wait_ge(s["sparsed"], i.through())
                pe.transpose(bank("st", i)[:, 0:P], sparse[:, i.par], ident).then_inc(s["st_ps"], 1)

            def spectrum(n):
                pe.wait_ge(s["tripled"], n.through())
                if n.static and n.k == 0:
                    pe.wait_ge(s["neg_made"], 1)
                else:
                    pe.wait_ge(s["filter_sb"], n.through(1))
                for j in range(4):
                    last = pe.matmul(ps_spec[:, :], neg_hartley[:, :] if j else hartley, triple[:, j],
                                     start=(j == 0), stop=(j == 3))
                last.then_inc(s["spec_ps"], 1)

            def output(n, which, pieces, lhs):
                bias = bias_parts[:, bass.ds(n.layer * E + which * LAYERS * E, E)]
                bias = bias.rearrange("p (o e) -> p o e", o=1).broadcast_to((P, T, E))
                pe.matmul(ps_out[:, :].rearrange("p (t e) -> p t e", t=T), ones_3[:, :], bias, start=True, stop=False,
                          skip_group_check=True)
                for i in range(T):
                    for k, w in enumerate(pieces):
                        last = pe.matmul(ps_out[:, i * E:(i + 1) * E], lhs(k, i), w, start=False,
                                         stop=(k == len(pieces) - 1), skip_group_check=True)
                return last

            def projection(n):
                pe.wait_ge(s["filter_sb"], n.through())
                out_free("proj", n)
                output(n, 0, [w_rproj[:, bass.ds(n.layer * E, E)]],
                       lambda k, i: filtered[:, i * P:(i + 1) * P]).then_inc(s["attn_ps"], 1)

            def full_product(i):
                pe.wait_ge(s["xhat_sb"], i.through())
                out_free("ffn1", i)
                pe.matmul(ps_out[:, 0:E], x_hatT[:, i.par], w_ffn[:, :], start=True, stop=True, skip_group_check=True)

            def sparse_product(i):
                pe.matmul(ps_out[:, E:2 * E], ones_3[:, :], bias_parts[:, 2 * LAYERS * E:NBIAS], start=True, stop=False,
                          skip_group_check=True)
                pe.wait_ge(s["st_sb"], i.through())
                pe.matmul(ps_out[:, E:2 * E], sparseT[:, i.par], w_ffn[:, :], start=False, stop=True,
                          skip_group_check=True).then_inc(s["ffn_ps"], 1)

            def mlp(n):
                for k in range(FK):
                    pe.wait_ge(s[f"fc{k}_sb"], n.through())
                out_free("mlp", n)
                output(n, 1, [w_mlp[:, bass.ds(n.layer * (FK * E) + k * E, E)] for k in range(FK)],
                       lambda k, i: hidden[:, k, i * P:(i + 1) * P]).then_inc(s["mlp_ps"], 1)

            pe.wait_ge(s["linb_in"], 32)
            pe.wait_ge(s["const_made"], 1)
            pe.wait_ge(s["ffnw_in"], 16)
            pe.wait_ge(s["wmlp_in"], 16)
            pe.wait_ge(s["bias_lo"], 1)

            def slot(at):
                at(1, t2)
                at(2, spectrum)
                at(1, fc, 1)
                at(4, t1)
                at(2, projection)
                at(1, fc, 0)
                at(4, qkv, 0)
                at(4, qkv, 2)
                at(4, qkv, 1)
                at(1, sparse_t)
                at(1, full_product)
                at(4, qkv_diff, 0)
                at(1, fc, 2)
                at(1, sparse_product)
                at(1, fc, 3)
                at(4, qkv_diff, 2)
                at(4, qkv_diff, 1)
                at(1, mlp)
                at(3, scores)

            run_slots(pe, slot)

        @block.scalar
        def _(act):
            def filled(name, n):
                act.wait_ge(s[name + "_ps"], n.through())
                return ps_rot[:, [x for x, _ in FILLS].index(name) % 2]

            def empty(dst, name, src, func=ACT.Copy, **how):
                act.activation(dst, src, func, **how).then_inc(s[name + "_sb"], 1)

            starts = 0

            def start_filled():
                nonlocal starts
                starts += 1
                act.wait_ge(s["start_ps"], starts)
                return ps_rot[:, (starts - 1) % 2]

            empty(par_all[:, :], "start", start_filled()[:, 0:LAYERS * NPAR])
            lin = start_filled()
            act.wait_ge(s["w_lin_zero"], 1)
            act.activation(w_lin[0:G, 0:E], lin[0:G, 0:P], ACT.Copy)
            empty(w_lin[G:2 * G, E:2 * E], "start", lin[G:2 * G, 0:P])
            act.wait_ge(s["bott_in"], 6 * 16)
            for b in range(B):
                empty((h1, h2)[b % 2][:, :], "start", start_filled())
                empty(conv_out[:, b * S:(b + 1) * S], "start", start_filled()[0:2 * G], ACT.Identity, bias=bott[:, 0:1])
            empty(w_rproj[:, :], "start", start_filled())
            act.wait_ge(s["bias_in"], 9 * 16)
            act.activation(bias_parts[:, :], bias_rows[:, :], ACT.Copy).then_inc(s["bias_hi"], 1)
            act.wait_ge(s["bias_rem"], 1)
            act.activation(bias_parts[64:P, :], bias_rest[64:P, :], ACT.Copy).then_inc(s["bias_mid"], 1)
            act.wait_ge(s["wqkv_in"], 16)

            def layer_vectors(dst, base, first, width, done):
                act.activation(dst[:, :], par_all[:, bass.ds(base * NPAR + first, width)], ACT.Copy).then_inc(done, 1)

            def normalise(n, which):
                act.wait_ge(s[f"ln{which}_shift"], n.through())
                if not n.static or n.k:
                    act.wait_ge(s[f"t{which}_ps"], n.through(1))
                for i in range(T):
                    c = T * n.b + i
                    last = act.activation(normed[:, which - 1, i], x_stream[:, c], ACT.Identity,
                                          scale=rstd[which][:, c:c + 1], bias=shift[which][:, c:c + 1])
                last.then_inc(s[f"ln{which}_norm"], 1)

            def h1_empty(n):
                if n.b == 0:
                    layer_vectors(par_ln1, n.layer, LN1W, 2, s["par_ln1_r"])
                    act.wait_ge(s["par_ln1_r"], n.layer + 1)
                if not n.static or n.k:
                    for j in "qkv":
                        act.wait_ge(s[j + "_ps"], n.through(1))
                    act.wait_ge(s["diffed"], n.through(1))
                empty(h1[:, :], "t1", filled("t1", n), ACT.Identity, bias=par_ln1[:, 1:2], scale=par_ln1[:, 0:1])

            def sort_columns(n):
                if n.b == 0:
                    layer_vectors(par_qkv, n.layer, QKVB, 3, s["par_qkv_r"])
                    act.activation(w_qkv[:, :].rearrange("p j (h d) -> p j h d", d=HD),
                                   w_qkv_raw[:, bass.ds(n.layer * (3 * E), 3 * E)].rearrange("p (h j d) -> p j h d", j=3, d=HD),
                                   ACT.Copy).then_inc(s["wqkv_sb"], 1)

            def buffer_free(n):
                if not n.static or n.k >= 2:
                    act.wait_ge(s["tripled"], n.through(2))

            def qkv_empty(n, j):
                buffer_free(n)
                if n.b == 0:
                    act.wait_ge(s["par_qkv_r"], n.layer + 1)
                name = "qkv"[j]
                empty(quat[:, n.par, 0, j], name, filled(name, n), ACT.Identity, bias=par_qkv[:, j:j + 1])

            def diff_empty(n, j):
                buffer_free(n)
                name = "qkv"[j] + "d"
                empty(quat[:, n.par, 1, j], name, filled(name, n))

            def count_turns(n):
                if not n.static or n.k:
                    act.wait_ge(s["fraced"], n.through(1))
                for j in "qkv":
                    act.wait_ge(s[j + "_sb"], n.through())
                act.activation(turns[:, :], quat[:, n.par, 0], ACT.Identity, bias=0.25, scale=INV_TURN).then_inc(s["turned"], 1)

            def round_turns(n):
                act.wait_ge(s["turned"], n.through())
                act.activation(frac[:, :], turns[:, :], ACT.Identity, bias=ROUND).then_inc(s["rounded"], 1)

            def cosine(n):
                act.wait_ge(s["fraced"], n.through())
                act.activation(quat[:, n.par, 3], frac[:, :], ACT.Sin, scale=-TURN).then_inc(s["cosined"], 1)

            def h2_empty(n):
                if n.b == 0:
                    layer_vectors(par_ln2, n.layer, LN2W, 2, s["par_ln2_r"])
                    act.wait_ge(s["par_ln2_r"], n.layer + 1)
                if not n.static or n.k:
                    for k in range(FK):
                        act.wait_ge(s[f"fc{k}_ps"], n.through(1))
                empty(h2[:, :], "t2", filled("t2", n), ACT.Identity, bias=par_ln2[:, 1:2], scale=par_ln2[:, 0:1])

            def gelu(n, k):
                if n.b == 0 and k == 1:
                    layer_vectors(par_fc, n.layer, FCB, FK, s["par_fc_r"])
                    act.wait_ge(s["par_fc_r"], n.layer + 1)
                if not n.static or n.k:
                    act.wait_ge(s["mlp_ps"], n.through(1))
                name = f"fc{k}"
                empty(hidden[:, k], name, filled(name, n), ACT.Gelu, bias=par_fc[:, k:k + 1])

            def ffn_gate(i):
                if i.static and i.k == 0:
                    act.wait_ge(s["bn_shift"], 1)
                src = conv_out[:, bass.ds(i.base * (B * P) + i.k * P, P)]
                act.activation(gate[0:2 * G, i.par], src, ACT.Gelu, bias=bn_sc[:, 3:4], scale=bn_sc[:, 1:2]).then_inc(s["gated"], 1)

            def scores_empty(i):
                room = filled("lg", i)
                if not i.static or i.k >= 2:
                    act.wait_ge(s["struck0"], i.count(2, 2 - 4))
                    act.wait_ge(s["ffn_ps"], i.through(2))
                act.activation(x_hatT[:, i.par], room[:, 2 * E:2 * E + P], ACT.Copy).then_inc(s["xhat_sb"], 1)
                empty(logits[:, i.par], "lg", room[:, 0:2 * E])

            def exponentials(i):
                act.wait_ge(s["negmax_r"], i.through())
                if not i.static or i.k >= 2:
                    act.wait_ge(s["kept_r"], i.through(2))
                for g in range(2):
                    act.activation(expd[:, i.par, g], logits[:, i.par, g], ACT.Exp,
                                   bias=neg_max[:, i.par, g:g + 1], accum_out=esum[:, i.par, g:g + 1]).then_inc(s["exped"], 1)

            def sparse_empty(i):
                empty(sparseT[:, i.par], "st", filled("st", i)[:, 0:P])

            def slot(at):
                at(4, normalise, 1)
                at(1, gelu, 1)
                at(4, sort_columns)
                at(4, h1_empty)
                at(3, ffn_gate)
                at(1, gelu, 0)
                at(4, qkv_empty, 0)
                at(4, qkv_empty, 2)
                at(4, qkv_empty, 1)
                at(1, sparse_empty)
                at(4, count_turns)
                at(4, diff_empty, 0)
                at(1, gelu, 2)
                at(4, round_turns)
                at(1, gelu, 3)
                at(4, diff_empty, 2)
                at(4, cosine)
                at(4, diff_empty, 1)
                at(2, normalise, 2)
                at(3, scores_empty)
                at(2, exponentials)
                at(2, h2_empty)

            run_slots(act, slot)

        @block.vector
        def _(dve):
            tt, ts, stt = dve.tensor_tensor, dve.tensor_scalar, dve.scalar_tensor_tensor
            pauses = 0

            def take_waits():
                nonlocal pauses
                dve.memset(pause[:, pauses % 64:pauses % 64 + 1], 0.0)
                pauses += 1

            dve.memset(w_lin[:, :], 0.0).then_inc(s["w_lin_zero"], 1)
            dve.memset(ones_3[:, :], 0.0)
            dve.memset(bias_rows[:, :], 0.0).then_inc(s["zeroed"], 1)
            dve.wait_ge(s["zeroed"], 1)
            for row in PART_ROWS:
                dve.memset(ones_3[row:row + 1, :], 1.0)
            dve.memset(h_diff[:, 0:1], 0.0)
            dve.memset(gate[2 * G:2 * G + 1, :, :], 1.0).then_inc(s["const_made"], 1)

            def layer_stats(n, which, nth):
                raw, done = s[f"ln{which}_raw"], s[f"ln{which}_stats"]
                for i in range(T):
                    last = dve.bn_stats(stats[which][:, T * n.b + i], x_stream[:, T * n.b + i])
                last.then_inc(raw, 1)
                dve.wait_ge(raw, nth)
                take_waits()
                for i in range(T):
                    last = dve.bn_aggr(meanvar[which][:, T * n.b + i], stats[which][:, T * n.b + i])
                last.then_inc(done, 1)

            for b in range(B):
                dve.wait_ge(s[f"x{b}_in"], 16)
                for i in range(T):
                    last = dve.bn_stats(stats[0][:, T * b + i], x_in[:, T * b + i])
                last.then_inc(s["s0_raw"], 1)
                dve.wait_ge(s["s0_raw"], b + 1)
                for i in range(T):
                    last = dve.bn_aggr(meanvar[0][:, T * b + i], stats[0][:, T * b + i])
                last.then_inc(s["s0_mv"], 1)
            dve.wait_ge(s["conv_in"], 32)
            dve.wait_ge(s["const_in"], 16)
            for g in range(2):
                last = ts(w_conv[:, g * G:(g + 1) * G], group, conv_col[:, g:g + 1], None, ALU.mult)
            last.then_inc(s["convw_made"], 1)
            ts(neg_hartley[:, :], hartley, -1.0, None, ALU.mult).then_inc(s["neg_made"], 1)
            for b in range(B):
                dve.wait_ge(s["s0_rstd"], b + 1)
                for c in range(T * b, T * b + T):
                    last = ts(x_stream[:, c], x_in[:, c], meanvar[0][:, c, 0:1], rstd[0][:, c:c + 1], ALU.subtract, ALU.mult)
                last.then_inc(s["x0_ready"], 1)
                dve.wait_ge(s["x0_ready"], b + 1)
                layer_stats(Turn(0, b), 1, b + 1)

            for b in range(B):
                dve.wait_ge(s["start_sb"], 2 + 2 * b + 2)
                last = dve.bn_stats(bn_stats[:, b], conv_out[:, b * S:(b + 1) * S])
            last.then_inc(s["bn_raw"], 1)
            dve.wait_ge(s["bn_raw"], 1)
            dve.bn_aggr(bn_mv[:, :], bn_stats[:, :]).then_inc(s["bn_mv_r"], 1)
            dve.wait_ge(s["bn_rstd"], 1)
            tt(bn_sc[:, 1:2], bott[:, 1:2], bn_sc[:, 0:1], ALU.mult).then_inc(s["bn_scale_r"], 1)
            dve.wait_ge(s["bn_scale_r"], 1)
            tt(bn_sc[:, 2:3], bn_mv[:, 0:1], bn_sc[:, 1:2], ALU.mult).then_inc(s["bn_ms_r"], 1)
            dve.wait_ge(s["bn_ms_r"], 1)
            tt(bn_sc[:, 3:4], bott[:, 2:3], bn_sc[:, 2:3], ALU.subtract).then_inc(s["bn_shift"], 1)

            def whole_turns(n):
                dve.wait_ge(s["rounded"], n.through())
                stt(frac[:, :], frac[:, :], ROUND, turns[:, :], ALU.subtract, ALU.subtract).then_inc(s["fraced"], 1)

            def ffn_hat(i):
                at = i.base * B + i.k
                if not i.static or i.k >= 2:
                    dve.wait_ge(s["lg_ps"], i.through(2))
                    take_waits()
                ts(x_hat[:, i.par], x_flat[:, bass.ds(at * E, E)],
                   meanvar[0][:, :, :].rearrange("p t c -> p (t c)")[:, bass.ds(at * 2, 1)],
                   rstd[0][:, bass.ds(at, 1)], ALU.subtract, ALU.mult).then_inc(s["hatted"], 1)

            def quaternions(engine, n):
                for j in "qk":
                    engine.wait_ge(s[j + "d_sb"], n.through())
                engine.wait_ge(s["cosined"], n.through())
                engine.wait_ge(s[f"rolled{n.par}"], n.pairs(32, 32))

            def taken(n, *terms):
                if not n.static or n.k:
                    for term in terms:
                        dve.wait_ge(s[term], n.through(1))

            def square_01(n):
                a, b = quat[:, n.par, :, 0], quat[:, n.par, :, 1]
                quaternions(dve, n)
                taken(n, "c0a_r", "c1b_r")
                tt(square01[:, :], a[:, 0:2], b[:, 0:2], ALU.mult).then_inc(s["sq01_r"], 1)

            def c23_first(n):
                a, b = quat[:, n.par, :, 0], quat[:, n.par, :, 1]
                quaternions(dve, n)
                taken(n, "tripled")
                tt(ps_c[:, 2:4], a[:, 0:1].broadcast_to((P, 2, S)), b[:, 2:4], ALU.mult).then_inc(s["c23a_r"], 1)

            def c0_first(n):
                dve.wait_ge(s["sq01_r"], n.through())
                taken(n, "tripled")
                tt(ps_c[:, 0], square01[:, 0], square01[:, 1], ALU.subtract).then_inc(s["c0a_r"], 1)

            def c1_first(n):
                dve.wait_ge(s["sq01_r"], n.through())
                taken(n, "tripled")
                dve.memset(ps_c[:, 1, 0:1], 0.0)
                tt(ps_c[:, 1, 1:S], square01[:, 0, 1:S], square01[:, 0, 0:S - 1], ALU.subtract).then_inc(s["c1a_r"], 1)

            def c23_second(n):
                dve.wait_ge(s["c23a_r"], n.through())
                dve.wait_ge(s["p20_r"], n.through())
                tt(ps_c[:, 2:4], ps_c[:, 2:4], prod_20[:, :], ALU.add).then_inc(s["c23b_r"], 1)

            def c1_second(n):
                dve.wait_ge(s["c1a_r"], n.through())
                tt(ps_c[:, 1], ps_c[:, 1], square01[:, 1], ALU.add).then_inc(s["c1b_r"], 1)

            def c0_second(n):
                dve.wait_ge(s["c0a_r"], n.through())
                dve.wait_ge(s["sq23_r"], n.through())
                tt(ps_c[:, 0], ps_c[:, 0], sum23[:, :], ALU.subtract).then_inc(s["c0_made"], 1)

            def c1_third(n):
                dve.wait_ge(s["c1b_r"], n.through())
                dve.wait_ge(s["p23_r"], n.through())
                tt(ps_c[:, 1], ps_c[:, 1], prod_23[:, 0], ALU.add).then_inc(s["c1c_r"], 1)

            def c1_last(n):
                dve.wait_ge(s["c1c_r"], n.through())
                tt(ps_c[:, 1], ps_c[:, 1], prod_23[:, 1], ALU.subtract).then_inc(s["c1_made"], 1)

            def c23_last(n):
                dve.wait_ge(s["c23b_r"], n.through())
                dve.wait_ge(s["crossed"], n.through())
                tt(ps_c[:, 2:4], ps_c[:, 2:4], cross[:, :], ALU.add).then_inc(s["c23_made"], 1)

            def triple_products(n):
                dve.wait_ge(s["vd_sb"], n.through())
                for made in ("c0_made", "c1_made", "c23_made"):
                    dve.wait_ge(s[made], n.through())
                if not n.static or n.k:
                    dve.wait_ge(s["spec_ps"], n.through(1))
                tt(triple[:, :], ps_c[:, :], quat[:, n.par, :, 2], ALU.mult).then_inc(s["tripled"], 1)

            def spectrum_gain(n):
                dve.wait_ge(s["spec_ps"], n.through())
                if not n.static or n.k:
                    dve.wait_ge(s["attn_ps"], n.through(1))
                tt(filtered[:, :], ps_spec[:, :], gain, ALU.mult).then_inc(s["filter_sb"], 1)

            out_tiles = ps_out[:, :].rearrange("p (t e) -> p t e", t=T)

            def add_attention(n):
                x = x_stream[:, n.tiles]
                dve.wait_ge(s["attn_ps"], n.through())
                tt(x, out_tiles, x, ALU.add).then_inc(s["x_mid"], 1)

            def stats_2(n):
                dve.wait_ge(s["x_mid"], n.through())
                layer_stats(n, 2, n.through())

            def add_mlp(n):
                x = x_stream[:, n.tiles]
                dve.wait_ge(s["mlp_ps"], n.through())
                tt(x, out_tiles, x, ALU.add).then_inc(s["x_ready"], 1)

            def stats_1(n):
                if not (n.static and n.layer == LAYERS - 1):
                    dve.wait_ge(s["x_ready"], n.through())
                    layer_stats(n, 1, n.through(-B))

            def finish(n):
                if n.static and n.layer == LAYERS - 1:
                    dve.wait_ge(s["x_ready"], n.through())
                    dve.wait_ge(s["acc_made"], T * n.b + T)
                    if n.b >= 2:
                        dve.wait_ge(s[f"out{n.par}_out"], 16)
                    tt(result[:, n.par], x_stream[:, n.tiles], x_in[:, n.tiles], ALU.add).then_inc(s["resulted"], 1)

            def take_top(i, r):
                if r:
                    dve.wait_ge(s[f"struck{r - 1}"], i.count(2, 2))
                else:
                    dve.wait_ge(s["lg_sb"], i.through())
                take_waits()
                for g in range(2):
                    dve.max(top[:, i.par, g], (left if r else logits)[:, i.par, g]).then_inc(s[f"topped{r}"], 1)

            def negate_max(i):
                dve.wait_ge(s["topped0"], i.count(2, 2))
                if not i.static or i.k >= 2:
                    dve.wait_ge(s["exped"], i.count(2, 2 - 4))
                ts(neg_max[:, i.par, :], top[:, i.par, :, 0], -1.0, None, ALU.mult).then_inc(s["negmax_r"], 1)

            def strike(i, r):
                dve.wait_ge(s[f"topped{r}"], i.count(2, 2))
                take_waits()
                for g in range(2):
                    dve.match_replace(left[:, i.par, g], top[:, i.par, g], (left if r else logits)[:, i.par, g],
                                      SELECTED).then_inc(s[f"struck{r}"], 1)

            def keep(i):
                p = i.par
                dve.wait_ge(s["exped"], i.count(2, 2))
                dve.reciprocal(rsum[:, p, :], esum[:, p, :]).then_inc(s["rsum_r"], 1)
                dve.wait_ge(s["struck3"], i.count(2, 2))
                stt(kept[:, p], left[:, p], SELECTED, expd[:, p], ALU.is_equal, ALU.mult).then_inc(s["kept_r"], 1)
                dve.wait_ge(s["rsum_r"], i.through())
                dve.wait_ge(s["kept_r"], i.through())
                stt(sparse[:, p], kept[:, p, 1], rsum[:, p, 1:2], x_hat[:, p], ALU.mult, ALU.mult).then_inc(s["sparsed"], 1)

            def ffn_add(i):
                p = i.par
                x = x_flat[:, bass.ds((i.base * B + i.k) * E, E)]
                dve.wait_ge(s["ffn_ps"], i.through())
                stt(branch[:, p], kept[:, p, 0], rsum[:, p, 0:1], ps_out[:, 0:E], ALU.mult, ALU.mult).then_inc(s["branched"], 1)
                tt(branch_x[:, p], ps_out[:, E:2 * E], x, ALU.add).then_inc(s["branch_xed"], 1)
                dve.wait_ge(s["branched"], i.through())
                dve.wait_ge(s["branch_xed"], i.through())
                tt(x, branch_x[:, p], branch[:, p], ALU.add).then_inc(s["acc_made"], 1)

            def slot(at):
                at(1, ffn_add)
                at(3, c23_last)
                at(4, whole_turns)
                at(3, c0_second)
                at(2, take_top, 2)
                at(3, triple_products)
                at(0, finish)
                at(2, strike, 2)
                at(1, add_mlp)
                at(1, stats_1)
                at(4, square_01)
                at(3, take_top, 0)
                at(4, c0_first)
                at(4, c1_first)
                at(2, take_top, 3)
                at(4, c1_second)
                at(3, negate_max)
                at(3, spectrum_gain)
                at(2, strike, 3)
                at(4, c1_third)
                at(2, keep)
                at(3, strike, 0)
                at(4, c1_last)
                at(3, add_attention)
                at(4, c23_first)
                at(3, take_top, 1)
                at(4, c23_second)
                at(3, strike, 1)
                at(3, stats_2)
                at(4, ffn_hat)

            run_slots(dve, slot)

        @block.gpsimd
        def _(pool):
            tt, ts = pool.tensor_tensor, pool.tensor_scalar
            pool.memset(eps_tile[:, :], EPS)
            pool.memset(zeros[:, :], 0.0)
            pool.memset(minus_half[:, :], -0.5)
            pool.drain()

            def inverse_std(which, b, name, nth):
                c = slice(T * b, T * b + T)
                pool.wait_ge(s[f"{name}_mv" if which == 0 else f"{name}_stats"], nth)
                tt(var_eps[which][:, c], meanvar[which][:, c, 1], eps_tile[:, :], ALU.add).then_inc(s[f"{name}_eps"], 1)
                pool.wait_ge(s[f"{name}_eps"], nth)
                tt(rstd[which][:, c], var_eps[which][:, c], minus_half[:, c], ALU.pow).then_inc(s[f"{name}_rstd"], 1)
                if which == 0:
                    return
                pool.wait_ge(s[f"{name}_rstd"], nth)
                tt(mean_rstd[which][:, c], meanvar[which][:, c, 0], rstd[which][:, c], ALU.mult).then_inc(s[f"{name}_mr"], 1)
                pool.wait_ge(s[f"{name}_mr"], nth)
                tt(shift[which][:, c], zeros[:, :], mean_rstd[which][:, c], ALU.subtract).then_inc(s[f"{name}_shift"], 1)

            def difference(n):
                pool.wait_ge(s["t1_sb"], n.through())
                if not n.static or n.k:
                    for j in "qkv":
                        pool.wait_ge(s[j + "d_ps"], n.through(1))
                tt(h_diff[:, 1:S], h1[:, 1:S], h1[:, 0:S - 1], ALU.subtract).then_inc(s["diffed"], 1)

            def pair(n):
                return quat[:, n.par, :, 0], quat[:, n.par, :, 1]

            def ready(n, taken=None):
                for j in "qk":
                    pool.wait_ge(s[j + "d_sb"], n.through())
                pool.wait_ge(s["cosined"], n.through())
                pool.wait_ge(s[f"rolled{n.par}"], n.pairs(32, 32))
                if taken and (not n.static or n.k):
                    pool.wait_ge(s[taken], n.through(1))

            def times_b0(n):
                a, b = pair(n)
                ready(n, "c23b_r")
                tt(prod_20[:, :], a[:, 2:4], b[:, 0:1].broadcast_to((P, 2, S)), ALU.mult).then_inc(s["p20_r"], 1)

            def square_23(n):
                a, b = pair(n)
                ready(n, "c0_made")
                tt(square23[:, :], a[:, 2:4], b[:, 2:4], ALU.mult).then_inc(s["sq23_raw"], 1)
                pool.wait_ge(s["sq23_raw"], n.through())
                tt(sum23[:, :], square23[:, 0], square23[:, 1], ALU.add).then_inc(s["sq23_r"], 1)

            def product_23(n):
                a, b = pair(n)
                ready(n, "c1_made")
                tt(prod_23[:, 0], a[:, 2], b[:, 3], ALU.mult)
                tt(prod_23[:, 1], a[:, 3], b[:, 2], ALU.mult).then_inc(s["p23_r"], 1)

            def cross_1a(n):
                a, b = pair(n)
                ready(n)
                if not n.static or n.k:
                    pool.wait_ge(s["crossed"], n.through(1))
                tt(cross_a[:, :], a[:, 1:2].broadcast_to((P, 2, S)), b[:, 2:4], ALU.mult).then_inc(s["crossa_r"], 1)

            def cross_1b(n):
                a, b = pair(n)
                ready(n)
                if not n.static or n.k:
                    pool.wait_ge(s["crossed"], n.through(1))
                tt(cross_b[:, :], a[:, 2:4], b[:, 1:2].broadcast_to((P, 2, S)), ALU.mult).then_inc(s["crossb_r"], 1)

            def cross_terms(n):
                pool.wait_ge(s["crossa_r"], n.through())
                pool.wait_ge(s["crossb_r"], n.through())
                if not n.static or n.k:
                    pool.wait_ge(s["c23_made"], n.through(1))
                tt(cross[:, 0], cross_b[:, 1], cross_a[:, 1], ALU.subtract)
                tt(cross[:, 1], cross_a[:, 0], cross_b[:, 0], ALU.subtract).then_inc(s["crossed"], 1)

            def rstd_1(n):
                if not (n.static and n.layer == LAYERS - 1):
                    inverse_std(1, n.b, "ln1", n.through(-B))

            def rstd_2(n):
                inverse_std(2, n.b, "ln2", n.through())

            for b in range(B):
                inverse_std(0, b, "s0", b + 1)
            for b in range(B):
                inverse_std(1, b, "ln1", b + 1)
            pool.wait_ge(s["bn_mv_r"], 1)
            tt(bn_sc[:, 2:3], bn_mv[:, 1:2], eps_tile[0:2 * G, 0:1], ALU.add).then_inc(s["bn_eps_r"], 1)
            pool.wait_ge(s["bn_eps_r"], 1)
            tt(bn_sc[:, 0:1], bn_sc[:, 2:3], minus_half[0:2 * G, 0:1], ALU.pow).then_inc(s["bn_rstd"], 1)
            pool.wait_ge(s["bias_hi"], 1)
            tt(bias_rest[:, :], bias_rows[:, :], bias_parts[:, :], ALU.subtract).then_inc(s["bias_rem"], 1)
            pool.wait_ge(s["bias_mid"], 1)
            tt(bias_parts[96:P, :], bias_rest[96:P, :], bias_parts[96:P, :], ALU.subtract).then_inc(s["bias_lo"], 1)

            def slot(at):
                at(1, rstd_2)
                at(3, product_23)
                at(0, rstd_1)
                at(3, times_b0)
                at(3, cross_1a)
                at(3, cross_1b)
                at(4, difference)
                at(3, cross_terms)
                at(3, square_23)

            run_slots(pool, slot)


_INS = (["L0_attn_" + n for n in ("x", "ln1_w", "ln1_b", "attn_w", "attn_b", "aproj_w", "aproj_b", "ln2_w", "ln2_b",
                                  "fc_w", "fc_b", "mproj_w", "mproj_b")]
        + ["L0_ffn_weight", "L0_ffn_bias"]
        + [f"L0_ffn_{g}_{n}" for g in ("so", "si") for n in ("conv_w", "conv_b", "gamma", "beta", "lin_w", "lin_b")])


def kernel(**inputs):
    import numpy as _np
    import concourse.bacc as _bacc
    from concourse import mybir as _mybir
    from concourse.bass_utils import run_bass_kernel_spmd as _run

    nc = _bacc.Bacc("TRN2", target_bir_lowering=False, num_devices=1)
    arrays, aps = {}, {}
    for name in _INS:
        a = _np.ascontiguousarray(inputs[name])
        arrays[f"in_{name}_dram"] = a
        aps[name] = nc.dram_tensor(f"in_{name}_dram", a.shape, _mybir.dt.from_np(a.dtype), kind="ExternalInput").ap()
    c = shape_constants()
    arrays["shape_constants_dram"] = c
    consts = nc.dram_tensor("shape_constants_dram", c.shape, _mybir.dt.float32, kind="ExternalInput").ap()
    out = nc.dram_tensor("out_0_dram", (B, S, E), _mybir.dt.float32, kind="ExternalOutput").ap()
    build(nc, aps, consts, out)
    r = _run(nc, [arrays], core_ids=[0])
    return r.results[0]["out_0_dram"]
```

```python
from contextlib import ExitStack

import numpy as np

import concourse.bass as bass
from concourse import mybir

F32 = mybir.dt.float32
BF16 = mybir.dt.bfloat16
ALU = mybir.AluOpType
ACT = mybir.ActivationFunctionType

P = 128
B, S, E = 4, 512, 128
H, HD = 16, 8
LAYERS = 4
T = S // P
NT = B * T
FF = 4 * E
FK = FF // P
G = E // 4
TOPK = 32
EPS = 1e-5
TURN = 6.283185
INV_TURN = 1.0 / (2.0 * np.pi)
ROUND = 12582912.0
SELECTED = -3.0e38
NPAR = 11
LN1W, LN1B, QKVB, LN2W, LN2B, FCB = 0, 1, 2, 5, 6, 7
C_R, C_ID, C_GAIN, C_GROUP = 0, 128, 256, 768
NCONST = C_GROUP + G
NBIAS = 2 * LAYERS * E + E
PART_ROWS = (0, 64, 96)


def shape_constants():
    def cas(n):
        a = 2.0 * np.pi * np.outer(np.arange(n), np.arange(n)) / n
        return np.cos(a) + np.sin(a)
    c = np.zeros((P, NCONST), np.float64)
    c[:, C_R:C_R + E] = np.kron(cas(H), cas(HD)) / np.sqrt(E)
    c[:, C_ID:C_ID + P] = np.eye(P)
    kh = np.fft.fftfreq(H)[:, None, None]
    kd = np.fft.fftfreq(HD)[None, :, None]
    ks = np.fft.fftfreq(S)[None, None, :]
    km = np.sqrt(ks ** 2 + kh ** 2 + kd ** 2 + 1e-10)
    gain = np.cos(np.arctan(np.log(km + 1e-10))).reshape(E, S)
    lam = np.arange(S) / S
    t = np.arange(S) * 0.1
    mod = np.sin(t + lam) * np.cos(t - 2.0 * lam + 0.5 * lam ** 2)
    c[:, C_GAIN:C_GAIN + S] = gain * (1.0 + 0.1 * mod)
    c[:, C_GROUP:C_GROUP + G] = (np.arange(P)[:, None] // 4 == np.arange(G)[None, :])
    return c.astype(np.float32)


class Turn:

    def __init__(self, layer, k):
        self.base, self.k = layer, k
        self.static = isinstance(layer, int)
        self.layer = layer + k // B if k // B else layer
        self.b = k % B
        self.par = k % 2
        self.tiles = slice(T * self.b, T * self.b + T)

    def plus(self, d):
        return Turn(self.base, self.k + d)

    def exists(self):
        return not self.static or 0 <= self.k < NT // T * LAYERS

    def through(self, ago=0):
        return self.count(1, 1 - ago)

    def count(self, per=1, plus=0):
        assert self.static or self.k * per + plus > 0
        return self.base * (B * per) + (self.k * per + plus)

    def pairs(self, per, plus=0):
        assert self.static or self.k // 2 * per + plus > 0
        return self.base * (B // 2 * per) + (self.k // 2 * per + plus)


FILLS = [("t1", 4), ("fc2", 1), ("q", 4), ("v", 4), ("k", 4), ("st", 1), ("fc3", 1), ("lg", 3), ("kd", 4),
         ("vd", 4), ("t2", 2), ("qd", 4), ("fc0", 2), ("fc1", 2)]
OUTS = [("proj", 2), ("ffn1", 1), ("mlp", 1)]
OUT_READ = {"proj": "x_mid", "ffn1": "acc_made", "mlp": "x_ready"}
AHEAD = 4

FILL_COUNT = len(FILLS)
assert FILL_COUNT % 2 == 0
SLOTS = B * LAYERS


def step_before(order, stride, name, n):
    names = [x for x, _ in order]
    at = names.index(name)
    slot = n.plus(-order[at][1])
    for _ in range(SLOTS * len(order)):
        at -= stride
        if at < 0:
            at += len(order)
            slot = slot.plus(-1)
        other = slot.plus(order[at][1])
        if other.exists():
            return names[at], other
    return None


def build(nc, t, consts, out):
    with ExitStack() as ctx:
        def sb(name, shape, dt=F32):
            return ctx.enter_context(nc.sbuf_tensor(name, shape, dt))

        def psum(name, shape):
            return ctx.enter_context(nc.psum_tensor(name, shape, F32))

        def sem(name):
            return ctx.enter_context(nc.semaphore(name))

        const = sb("const", [P, NCONST])
        hartley = const[:, C_R:C_R + E]
        ident = const[:, C_ID:C_ID + P]
        gain = const[:, C_GAIN:C_GAIN + S]
        group = const[:, C_GROUP:C_GROUP + G]
        neg_hartley = sb("neg_hartley", [P, E])
        pause = sb("pause", [P, 64])
        eps_tile = sb("eps_tile", [P, T])
        zeros = sb("zeros", [P, T])
        minus_half = sb("minus_half", [P, NT])
        x_in = sb("x_in", [P, NT, E])
        x_flat = x_in[:, :, :].rearrange("p t e -> p (t e)")
        x_stream = sb("x_stream", [P, NT, E])
        par_rows = sb("par_rows", [LAYERS * NPAR, P])
        par_all = sb("par_all", [P, LAYERS * NPAR])
        par_ln1 = sb("par_ln1", [P, 2])
        par_qkv = sb("par_qkv", [P, 3])
        par_ln2 = sb("par_ln2", [P, 2])
        par_fc = sb("par_fc", [P, FK])
        bias_parts = sb("bias_parts", [P, NBIAS], BF16)
        ones_3 = sb("ones_3", [P, P], BF16)
        w_qkv_raw = sb("w_qkv_raw", [P, LAYERS * 3 * E])
        w_qkv = sb("w_qkv", [P, 3, E])
        w_fc = sb("w_fc", [P, FF])
        w_mlp = sb("w_mlp", [P, LAYERS * FK * E])
        w_rproj = sb("w_rproj", [P, LAYERS * E])
        stats = [sb(f"stats{i}", [P, NT, 6]) for i in range(3)]
        meanvar = [sb(f"meanvar{i}", [P, NT, 2]) for i in range(3)]
        var_eps = [sb(f"var_eps{i}", [P, NT]) for i in range(3)]
        rstd = [sb(f"rstd{i}", [P, NT]) for i in range(3)]
        mean_rstd = [sb(f"mean_rstd{i}", [P, NT]) for i in range(3)]
        shift = [sb(f"shift{i}", [P, NT]) for i in range(3)]
        normed = sb("normed", [P, 2, T, E])
        h1 = sb("h1", [P, S])
        h2 = sb("h2", [P, S])
        h_diff = sb("h_diff", [P, S])
        quat = sb("quat", [P, 2, 4, 3, S])
        turns = sb("turns", [P, 3, S])
        frac = sb("frac", [P, 3, S])
        square01 = sb("square01", [P, 2, S])
        square23 = sb("square23", [P, 2, S])
        sum23 = sb("sum23", [P, S])
        prod_20 = sb("prod_20", [P, 2, S])
        prod_23 = sb("prod_23", [P, 2, S])
        cross_a = sb("cross_a", [P, 2, S])
        cross_b = sb("cross_b", [P, 2, S])
        cross = sb("cross", [P, 2, S])
        triple = sb("triple", [P, 4, S])
        filtered = sb("filtered", [P, S])
        hidden = sb("hidden", [P, FK, S])
        w_proj = hidden[:, 0]
        bias_rest = hidden[:, 1:FK].rearrange("p k s -> p (k s)")[:, 0:NBIAS]
        bias_rows = triple[:, :].rearrange("p j s -> p (j s)")[:, 0:NBIAS]
        result = sb("result", [P, 2, T, E])
        conv_col = sb("conv_col", [P, 2])
        w_conv = sb("w_conv", [P, 2 * G])
        bott = sb("bott", [2 * G, 4])
        conv_out = sb("conv_out", [2 * G, B * S])
        gate = sb("gate", [2 * G + 1, 2, P])
        lin_rows = sb("lin_rows", [P, 2 * G])
        w_lin = sb("w_lin", [2 * G + 1, 2 * E])
        w_ffn = sb("w_ffn", [P, E])
        bn_stats = sb("bn_stats", [2 * G, B, 6])
        bn_mv = sb("bn_mv", [2 * G, 2])
        bn_sc = sb("bn_sc", [2 * G, 4])
        x_norm = sb("x_norm", [P, NT, E])
        x_norm_flat = x_norm[:, :, :].rearrange("p t e -> p (t e)")
        x_normT = sb("x_normT", [P, B * S])
        x_hatT = sb("x_hatT", [P, 2, P])
        logits = sb("logits", [P, 2, 2, E])
        left = sb("left", [P, 2, 2, E])
        top = sb("top", [P, 2, TOPK // 8, 2, 8])
        neg_max = sb("neg_max", [P, 2, 2])
        expd = sb("expd", [P, 2, 2, E])
        esum = sb("esum", [P, 2, 2])
        rsum = sb("rsum", [P, 2, 2])
        kept = sb("kept", [P, 2, 2, E])
        branch = sb("branch", [P, 2, E])
        sparse = sb("sparse", [P, 2, E])
        sparseT = sb("sparseT", [P, 2, P])

        ps_rot = psum("ps_rot", [P, 2, S])
        ps_spec = psum("ps_spec", [P, S])
        ps_out = psum("ps_out", [P, S])
        ps_c = psum("ps_c", [P, 4, S])
        conv_banks = (ps_spec[:, :], ps_out[:, :], ps_rot[:, 0], ps_rot[:, 1])

        s = {name: sem(name) for name in (
            "x0_in x1_in x2_in x3_in const_in par_in wproj_in wqkv_in wfc_in wmlp_in bias_in conv_in lin_in "
            "bott_in ffnw_in linb_in out0_out out1_out rolled0 rolled1 "
            "const_made zeroed neg_made convw_made w_lin_zero bias_hi bias_rem bias_mid bias_lo "
            "par_ps par_sb xt_ps xt_sb conv_ps conv_sb lin_ps lin_sb rproj_ps rproj_sb "
            "s0_raw s0_mv s0_eps s0_rstd x0_ready x0_copied bn_raw bn_mv_r bn_eps_r bn_rstd "
            "bn_scale_r bn_ms_r bn_shift gated negmax_r exped rsum_r kept_r sparsed "
            "topped0 topped1 topped2 topped3 struck0 struck1 struck2 struck3 "
            "ffn_ps branched acc_made "
            "ln1_raw ln1_stats ln1_eps ln1_rstd ln1_mr ln1_shift ln1_norm "
            "ln2_raw ln2_stats ln2_eps ln2_rstd ln2_mr ln2_shift ln2_norm "
            "diffed turned rounded fraced cosined par_ln1_r par_qkv_r par_ln2_r par_fc_r wqkv_sb xhat_sb "
            "sq01_r sq23_raw sq23_r p20_r p23_r c1c_r crossa_r crossb_r crossed c23a_r c0a_r c1a_r c1b_r c23b_r "
            "c0_made c1_made c23_made tripled spec_ps filter_sb attn_ps x_mid mlp_ps x_ready resulted"
        ).split()}
        s.update({name + end: sem(name + end) for name, _ in FILLS for end in ("_ps", "_sb")})

        x_dram = t["L0_attn_x"].rearrange("b s e -> (b s) e").rearrange("(b t p) e -> b p t e", t=T, p=P)
        out_dram = out.rearrange("b s e -> (b s) e").rearrange("(b t p) e -> b p t e", t=T, p=P)
        fc_w_dram = t["L0_attn_fc_w"]

        def run_slots(engine, slot, rest_of_start=None, after=None):
            def write(u):
                def at(lag, step, *args):
                    if u.plus(lag).exists():
                        step(u.plus(lag), *args)
                        if u.static and u.k + lag == 0 and (step, *args) == after:
                            rest_of_start()
                slot(at)
            for k in range(-AHEAD, 0):
                write(Turn(0, k))
            with engine.Fori(0, LAYERS - 1) as layer:
                for k in range(B):
                    write(Turn(layer, k))
            for k in range(SLOTS - B, SLOTS):
                write(Turn(0, k))

        block = ctx.enter_context(nc.Block())

        @block.sync
        def _(sp):
            for b in range(B):
                sp.dma_start(x_in[:, T * b:T * b + T, :], x_dram[b]).then_inc(s[f"x{b}_in"], 16)
                if b == 0:
                    sp.dma_start(const[:, :], consts).then_inc(s["const_in"], 16)
            for row, name in ((LN1W, "ln1_w"), (LN1B, "ln1_b"), (LN2W, "ln2_w"), (LN2B, "ln2_b")):
                sp.dma_start(par_rows[row:row + NPAR * (LAYERS - 1) + 1:NPAR, :],
                             t["L0_attn_" + name]).then_inc(s["par_in"], 16)
            for j in range(3):
                sp.dma_start(
                    par_rows[QKVB + j:QKVB + j + NPAR * (LAYERS - 1) + 1:NPAR, :].rearrange("l (h d) -> l h d", d=HD),
                    t["L0_attn_attn_b"].rearrange("l (h j d) -> j l h d", j=3, d=HD)[j]).then_inc(s["par_in"], 16)
            for k in range(FK):
                sp.dma_start(par_rows[FCB + k:FCB + k + NPAR * (LAYERS - 1) + 1:NPAR, :],
                             t["L0_attn_fc_b"][:, k * P:(k + 1) * P]).then_inc(s["par_in"], 16)
            sp.dma_start(w_qkv_raw[:, :].rearrange("p (l n) -> p l n", l=LAYERS),
                         t["L0_attn_attn_w"].rearrange("l p n -> p l n")).then_inc(s["wqkv_in"], 16)
            for g, name in enumerate(("so", "si")):
                sp.dma_start(conv_col[:, g:g + 1],
                             t[f"L0_ffn_{name}_conv_w"].rearrange("g (f o) -> (g f) o", o=1)).then_inc(s["conv_in"], 16)
            sp.wait_ge(s["zeroed"], 1)
            for row in PART_ROWS:
                for w, name in enumerate(("aproj", "mproj")):
                    sp.dma_start(bias_rows[row:row + 1, w * LAYERS * E:(w + 1) * LAYERS * E],
                                 t[f"L0_attn_{name}_b"].rearrange("(o l) e -> o (l e)", o=1)).then_inc(s["bias_in"], 16)
                sp.dma_start(bias_rows[row:row + 1, 2 * LAYERS * E:NBIAS],
                             t["L0_ffn_bias"].rearrange("(o e) -> o e", o=1)).then_inc(s["bias_in"], 16)
            for c, vec in enumerate(("conv_b", "gamma", "beta")):
                for g, name in enumerate(("so", "si")):
                    sp.dma_start(bott[g * G:(g + 1) * G, c:c + 1],
                                 t[f"L0_ffn_{name}_{vec}"].rearrange("(g o) -> g o", o=1)).then_inc(s["bott_in"], 16)

            def rest_of_start():
                for g, name in enumerate(("so", "si")):
                    sp.dma_start(lin_rows[:, g * G:(g + 1) * G], t[f"L0_ffn_{name}_lin_w"]).then_inc(s["lin_in"], 16)
                sp.dma_start(w_proj[:, :].rearrange("p (l e) -> p l e", l=LAYERS),
                             t["L0_attn_aproj_w"].rearrange("l i e -> i l e")).then_inc(s["wproj_in"], 16)
                sp.dma_start(w_ffn[:, :], t["L0_ffn_weight"]).then_inc(s["ffnw_in"], 16)
                sp.wait_ge(s["w_lin_zero"], 1)
                for g, name in enumerate(("so", "si")):
                    sp.dma_start(w_lin[2 * G:2 * G + 1, g * E:(g + 1) * E],
                                 t[f"L0_ffn_{name}_lin_b"].rearrange("(o e) -> o e", o=1)).then_inc(s["linb_in"], 16)
                sp.dma_start(w_fc[:, :], fc_w_dram[0]).then_inc(s["wfc_in"], 16)
                sp.dma_start(w_mlp[:, :].rearrange("p (l k e) -> p l k e", l=LAYERS, k=FK),
                             t["L0_attn_mproj_w"].rearrange("l (k p) e -> p l k e", p=P)).then_inc(s["wmlp_in"], 16)

                for b in range(B):
                    sp.wait_ge(s["x0_ready"], b + 1)
                    sp.dma_start(x_stream[:, T * b:T * b + T], x_norm[:, T * b:T * b + T]).then_inc(s["x0_copied"], 16)

            def roll(n):
                q, r = quat[:, n.par, 0], quat[:, n.par, 2]
                for j in "qkv":
                    sp.wait_ge(s[j + "_sb"], n.through())
                done = s[f"rolled{n.par}"]
                sp.dma_start(r[HD:P], q[0:P - HD]).then_inc(done, 16)
                sp.dma_start(r[0:HD], q[P - HD:P]).then_inc(done, 16)

            def next_fc(n):
                if n.b == B - 1 and not (n.static and n.layer == LAYERS - 1):
                    for k in range(FK):
                        sp.wait_ge(s[f"fc{k}_ps"], n.through())
                    sp.dma_start(w_fc[:, :], fc_w_dram[bass.ds(n.layer + 1, 1)].rearrange("o p n -> p (o n)")).then_inc(s["wfc_in"], 16)

            def slot(at):
                at(4, roll)
                at(1, next_fc)

            run_slots(sp, slot, rest_of_start, (roll,))
            for b in range(B):
                sp.wait_ge(s["resulted"], b + 1)
                sp.dma_start(out_dram[b], result[:, b % 2]).then_inc(s[f"out{b % 2}_out"], 16)
            for par in range(2):
                sp.wait_ge(s[f"out{par}_out"], 32)

        @block.tensor
        def _(pe):
            def bank(name, n):
                before = step_before(FILLS, 2, name, n)
                if before:
                    pe.wait_ge(s[before[0] + "_sb"], before[1].through())
                if n.static and n.k == 1 and name == "t1":
                    pe.wait_ge(s["conv_sb"], B)
                return ps_rot[:, [x for x, _ in FILLS].index(name) % 2]

            def out_free(name, n):
                before = step_before(OUTS, 1, name, n)
                if before:
                    pe.wait_ge(s[OUT_READ[before[0]]], before[1].through())

            def transposes(dst, src):
                for i in range(T):
                    last = pe.transpose(dst[:, i * P:(i + 1) * P], src[:, i], ident)
                return last

            pe.wait_ge(s["const_in"], 16)

            def conv(b):
                pe.wait_ge(s["xt_sb"], b + 1)
                if b == 0:
                    pe.wait_ge(s["convw_made"], 1)
                if b == 1:
                    pe.wait_ge(s["par_sb"], 1)
                if b == 2:
                    for name in ("q", "k", "v", "qd", "kd", "vd"):
                        pe.wait_ge(s[name + "_sb"], 1)
                pe.matmul(conv_banks[b][0:2 * G], w_conv[:, :], x_normT[:, b * S:(b + 1) * S], start=True,
                          stop=True).then_inc(s["conv_ps"], 1)

            def rest_of_start():
                for b in range(B):
                    pe.wait_ge(s["x0_ready"], b + 1)
                    transposes(ps_c[:, b], x_norm[:, T * b:T * b + T]).then_inc(s["xt_ps"], 1)
                for b in range(B):
                    conv(b)
                pe.wait_ge(s["lin_in"], 32)
                pe.wait_ge(s["conv_sb"], 1)
                pe.transpose(ps_spec[0:2 * G, 0:P], lin_rows[:, :], ident).then_inc(s["lin_ps"], 1)
                pe.wait_ge(s["wproj_in"], 16)
                pe.wait_ge(s["conv_sb"], 2)
                pe.matmul(ps_out[:, :], hartley, w_proj[:, :], start=True, stop=True).then_inc(s["rproj_ps"], 1)

            def first(n, *loads):
                if n.static and n.k == 0:
                    for name, value in loads:
                        pe.wait_ge(s[name], value)

            def t1(n):
                pe.wait_ge(s["ln1_norm"], n.through())
                transposes(bank("t1", n), normed[:, 0]).then_inc(s["t1_ps"], 1)
                if n.static and n.k == 0:
                    pe.wait_ge(s["par_in"], 11 * 16)
                    pe.transpose(ps_out[:, 0:LAYERS * NPAR], par_rows[:, :],
                                 const[0:LAYERS * NPAR, C_ID:C_ID + LAYERS * NPAR]).then_inc(s["par_ps"], 1)

            def qkv(n, j):
                name = "qkv"[j]
                pe.wait_ge(s["t1_sb"], n.through())
                pe.wait_ge(s["wqkv_sb"], n.layer + 1)
                pe.matmul(bank(name, n), w_qkv[:, j], h1[:, :], start=True, stop=True).then_inc(s[name + "_ps"], 1)

            def qkv_diff(n, j):
                name = "qkv"[j] + "d"
                pe.wait_ge(s["diffed"], n.through())
                pe.wait_ge(s["wqkv_sb"], n.layer + 1)
                pe.matmul(bank(name, n), w_qkv[:, j], h_diff[:, :], start=True, stop=True).then_inc(s[name + "_ps"], 1)

            def t2(n):
                pe.wait_ge(s["ln2_norm"], n.through())
                transposes(bank("t2", n), normed[:, 1]).then_inc(s["t2_ps"], 1)

            def fc(n, k):
                name = f"fc{k}"
                pe.wait_ge(s["t2_sb"], n.through())
                pe.wait_ge(s["wfc_in"], n.layer * 16 + 16)
                pe.matmul(bank(name, n), w_fc[:, k * P:(k + 1) * P], h2[:, :], start=True, stop=True).then_inc(s[name + "_ps"], 1)

            def scores(i):
                room = bank("lg", i)
                first(i, ("lin_sb", 1), ("linb_in", 32), ("const_made", 1))
                pe.wait_ge(s["gated"], i.through())
                pe.matmul(room[:, 0:2 * E], gate[:, i.par], w_lin[:, :], start=True, stop=True).then_inc(s["lg_ps"], 1)

            def sparse_t(i):
                pe.wait_ge(s["sparsed"], i.through())
                pe.transpose(bank("st", i)[:, 0:P], sparse[:, i.par], ident).then_inc(s["st_ps"], 1)

            def spectrum(n):
                pe.wait_ge(s["tripled"], n.through())
                if n.static and n.k == 0:
                    pe.wait_ge(s["neg_made"], 1)
                    pe.wait_ge(s["lin_sb"], 1)
                else:
                    pe.wait_ge(s["filter_sb"], n.through(1))
                for j in range(4):
                    last = pe.matmul(ps_spec[:, :], neg_hartley[:, :] if j else hartley, triple[:, j],
                                     start=(j == 0), stop=(j == 3))
                last.then_inc(s["spec_ps"], 1)

            def output(n, which, pieces, lhs):
                bias = bias_parts[:, bass.ds(n.layer * E + which * LAYERS * E, E)]
                bias = bias.rearrange("p (o e) -> p o e", o=1).broadcast_to((P, T, E))
                pe.matmul(ps_out[:, :].rearrange("p (t e) -> p t e", t=T), ones_3[:, :], bias, start=True, stop=False,
                          skip_group_check=True)
                for i in range(T):
                    for k, w in enumerate(pieces):
                        last = pe.matmul(ps_out[:, i * E:(i + 1) * E], lhs(k, i), w, start=False,
                                         stop=(k == len(pieces) - 1), skip_group_check=True)
                return last

            def projection(n):
                pe.wait_ge(s["filter_sb"], n.through())
                out_free("proj", n)
                first(n, ("rproj_sb", 1), ("bias_lo", 1))
                output(n, 0, [w_rproj[:, bass.ds(n.layer * E, E)]],
                       lambda k, i: filtered[:, i * P:(i + 1) * P]).then_inc(s["attn_ps"], 1)

            def full_product(i):
                pe.wait_ge(s["xhat_sb"], i.through())
                out_free("ffn1", i)
                first(i, ("ffnw_in", 16), ("rproj_sb", 1), ("bias_lo", 1))
                pe.matmul(ps_out[:, 0:E], x_hatT[:, i.par], w_ffn[:, :], start=True, stop=True, skip_group_check=True)

            def sparse_product(i):
                pe.matmul(ps_out[:, E:2 * E], ones_3[:, :], bias_parts[:, 2 * LAYERS * E:NBIAS], start=True, stop=False,
                          skip_group_check=True)
                pe.matmul(ps_out[:, E:2 * E], ident, x_flat[:, bass.ds((i.base * B + i.k) * E, E)], start=False, stop=False,
                          skip_group_check=True)
                pe.wait_ge(s["st_sb"], i.through())
                pe.matmul(ps_out[:, E:2 * E], sparseT[:, i.par], w_ffn[:, :], start=False, stop=True,
                          skip_group_check=True).then_inc(s["ffn_ps"], 1)

            def mlp(n):
                for k in range(FK):
                    pe.wait_ge(s[f"fc{k}_sb"], n.through())
                out_free("mlp", n)
                first(n, ("wmlp_in", 16), ("bias_lo", 1))
                output(n, 1, [w_mlp[:, bass.ds(n.layer * (FK * E) + k * E, E)] for k in range(FK)],
                       lambda k, i: hidden[:, k, i * P:(i + 1) * P]).then_inc(s["mlp_ps"], 1)

            def slot(at):
                at(2, spectrum)
                at(4, t1)
                at(1, fc, 2)
                at(4, qkv, 0)
                at(4, qkv, 2)
                at(4, qkv, 1)
                at(1, sparse_t)
                at(2, projection)
                at(1, fc, 3)
                at(3, scores)
                at(1, full_product)
                at(1, sparse_product)
                at(4, qkv_diff, 1)
                at(4, qkv_diff, 2)
                at(1, mlp)
                at(2, t2)
                at(4, qkv_diff, 0)
                at(2, fc, 0)
                at(2, fc, 1)

            run_slots(pe, slot, rest_of_start, (qkv_diff, 0))

        @block.scalar
        def _(act):
            def filled(name, n):
                act.wait_ge(s[name + "_ps"], n.through())
                return ps_rot[:, [x for x, _ in FILLS].index(name) % 2]

            def empty(dst, name, src, func=ACT.Copy, **how):
                act.activation(dst, src, func, **how).then_inc(s[name + "_sb"], 1)

            def conv_empty(b):
                act.wait_ge(s["conv_ps"], b + 1)
                act.activation(conv_out[:, b * S:(b + 1) * S], conv_banks[b][0:2 * G], ACT.Identity,
                               bias=bott[:, 0:1]).then_inc(s["conv_sb"], 1)

            def rest_of_start():
                for b in range(B):
                    act.wait_ge(s["xt_ps"], b + 1)
                    act.activation(x_normT[:, b * S:(b + 1) * S], ps_c[:, b], ACT.Copy).then_inc(s["xt_sb"], 1)
                act.wait_ge(s["bott_in"], 6 * 16)
                for b in range(B):
                    conv_empty(b)
                act.wait_ge(s["w_lin_zero"], 1)
                act.wait_ge(s["lin_ps"], 1)
                act.activation(w_lin[0:G, 0:E], ps_spec[0:G, 0:P], ACT.Copy)
                act.activation(w_lin[G:2 * G, E:2 * E], ps_spec[G:2 * G, 0:P], ACT.Copy).then_inc(s["lin_sb"], 1)
                act.wait_ge(s["rproj_ps"], 1)
                act.activation(w_rproj[:, :], ps_out[:, :], ACT.Copy).then_inc(s["rproj_sb"], 1)

            def layer_vectors(dst, base, first, width, done):
                act.activation(dst[:, :], par_all[:, bass.ds(base * NPAR + first, width)], ACT.Copy).then_inc(done, 1)

            def normalise(n, which):
                act.wait_ge(s[f"ln{which}_shift"], n.through())
                if not n.static or n.k:
                    act.wait_ge(s[f"t{which}_ps"], n.through(1))
                for i in range(T):
                    c = T * n.b + i
                    x = x_norm if which == 1 and n.static and n.k < B else x_stream
                    last = act.activation(normed[:, which - 1, i], x[:, c], ACT.Identity,
                                          scale=rstd[which][:, c:c + 1], bias=shift[which][:, c:c + 1])
                last.then_inc(s[f"ln{which}_norm"], 1)
                if which == 1 and n.static and n.k == 0:
                    act.wait_ge(s["par_ps"], 1)
                    act.activation(par_all[:, :], ps_out[:, 0:LAYERS * NPAR], ACT.Copy).then_inc(s["par_sb"], 1)
                    act.wait_ge(s["par_sb"], 1)

            def h1_empty(n):
                if n.b == 0:
                    layer_vectors(par_ln1, n.layer, LN1W, 2, s["par_ln1_r"])
                    act.wait_ge(s["par_ln1_r"], n.layer + 1)
                if not n.static or n.k:
                    for j in "qkv":
                        act.wait_ge(s[j + "_ps"], n.through(1))
                    act.wait_ge(s["diffed"], n.through(1))
                empty(h1[:, :], "t1", filled("t1", n), ACT.Identity, bias=par_ln1[:, 1:2], scale=par_ln1[:, 0:1])

            def sort_columns(n):
                if n.static and n.k == 0:
                    act.wait_ge(s["wqkv_in"], 16)
                if n.b == 0:
                    layer_vectors(par_qkv, n.layer, QKVB, 3, s["par_qkv_r"])
                    act.activation(w_qkv[:, :].rearrange("p j (h d) -> p j h d", d=HD),
                                   w_qkv_raw[:, bass.ds(n.layer * (3 * E), 3 * E)].rearrange("p (h j d) -> p j h d", j=3, d=HD),
                                   ACT.Copy).then_inc(s["wqkv_sb"], 1)

            def buffer_free(n):
                if not n.static or n.k >= 2:
                    act.wait_ge(s["tripled"], n.through(2))

            def qkv_empty(n, j):
                buffer_free(n)
                if n.b == 0:
                    act.wait_ge(s["par_qkv_r"], n.layer + 1)
                name = "qkv"[j]
                empty(quat[:, n.par, 0, j], name, filled(name, n), ACT.Identity, bias=par_qkv[:, j:j + 1])

            def diff_empty(n, j):
                buffer_free(n)
                name = "qkv"[j] + "d"
                empty(quat[:, n.par, 1, j], name, filled(name, n))

            def count_turns(n):
                if not n.static or n.k:
                    act.wait_ge(s["fraced"], n.through(1))
                for j in "qkv":
                    act.wait_ge(s[j + "_sb"], n.through())
                act.activation(turns[:, :], quat[:, n.par, 0], ACT.Identity, bias=0.25, scale=INV_TURN).then_inc(s["turned"], 1)

            def round_turns(n):
                act.wait_ge(s["turned"], n.through())
                act.activation(frac[:, :], turns[:, :], ACT.Identity, bias=ROUND).then_inc(s["rounded"], 1)

            def cosine(n):
                act.wait_ge(s["fraced"], n.through())
                act.activation(quat[:, n.par, 3], frac[:, :], ACT.Sin, scale=-TURN).then_inc(s["cosined"], 1)

            def h2_empty(n):
                if n.b == 0:
                    layer_vectors(par_ln2, n.layer, LN2W, 2, s["par_ln2_r"])
                    act.wait_ge(s["par_ln2_r"], n.layer + 1)
                if not n.static or n.k:
                    for k in range(FK):
                        act.wait_ge(s[f"fc{k}_ps"], n.through(1))
                empty(h2[:, :], "t2", filled("t2", n), ACT.Identity, bias=par_ln2[:, 1:2], scale=par_ln2[:, 0:1])

            def gelu(n, k):
                if n.b == 0 and k == 0:
                    layer_vectors(par_fc, n.layer, FCB, FK, s["par_fc_r"])
                    act.wait_ge(s["par_fc_r"], n.layer + 1)
                if not n.static or n.k:
                    act.wait_ge(s["mlp_ps"], n.through(1))
                name = f"fc{k}"
                empty(hidden[:, k], name, filled(name, n), ACT.Gelu, bias=par_fc[:, k:k + 1])

            def ffn_gate(i):
                if i.static and i.k == 0:
                    act.wait_ge(s["bn_shift"], 1)
                src = conv_out[:, bass.ds(i.base * (B * P) + i.k * P, P)]
                act.activation(gate[0:2 * G, i.par], src, ACT.Gelu, bias=bn_sc[:, 3:4], scale=bn_sc[:, 1:2]).then_inc(s["gated"], 1)

            def scores_empty(i):
                room = filled("lg", i)
                if not i.static or i.k >= 2:
                    act.wait_ge(s["struck0"], i.count(2, 2 - 4))
                    act.wait_ge(s["ffn_ps"], i.through(2))
                empty(logits[:, i.par], "lg", room[:, 0:2 * E])
                act.activation(x_hatT[:, i.par], x_normT[:, bass.ds(i.base * (B * P) + i.k * P, P)],
                               ACT.Copy).then_inc(s["xhat_sb"], 1)

            def exponentials(i):
                act.wait_ge(s["negmax_r"], i.through())
                if not i.static or i.k >= 2:
                    act.wait_ge(s["kept_r"], i.through(2))
                for g in range(2):
                    act.activation(expd[:, i.par, g], logits[:, i.par, g], ACT.Exp,
                                   bias=neg_max[:, i.par, g:g + 1], accum_out=esum[:, i.par, g:g + 1]).then_inc(s["exped"], 1)

            def sparse_empty(i):
                empty(sparseT[:, i.par], "st", filled("st", i)[:, 0:P])

            def slot(at):
                at(3, diff_empty, 1)
                at(3, diff_empty, 2)
                at(1, normalise, 2)
                at(3, cosine)
                at(3, diff_empty, 0)
                at(1, h2_empty)
                at(2, exponentials)
                at(1, gelu, 0)
                at(4, normalise, 1)
                at(1, gelu, 1)
                at(4, sort_columns)
                at(4, h1_empty)
                at(1, gelu, 2)
                at(3, ffn_gate)
                at(4, qkv_empty, 0)
                at(4, qkv_empty, 2)
                at(4, qkv_empty, 1)
                at(1, sparse_empty)
                at(4, count_turns)
                at(1, gelu, 3)
                at(3, scores_empty)
                at(4, round_turns)

            run_slots(act, slot, rest_of_start, (diff_empty, 0))

        @block.vector
        def _(dve):
            tt, ts, stt = dve.tensor_tensor, dve.tensor_scalar, dve.scalar_tensor_tensor
            pauses = 0

            def take_waits():
                nonlocal pauses
                dve.memset(pause[:, pauses % 64:pauses % 64 + 1], 0.0)
                pauses += 1

            dve.memset(w_lin[:, :], 0.0).then_inc(s["w_lin_zero"], 1)
            dve.memset(ones_3[:, :], 0.0)
            dve.memset(bias_rows[:, :], 0.0).then_inc(s["zeroed"], 1)
            dve.wait_ge(s["zeroed"], 1)
            for row in PART_ROWS:
                dve.memset(ones_3[row:row + 1, :], 1.0)
            dve.memset(h_diff[:, 0:1], 0.0)
            dve.memset(gate[2 * G:2 * G + 1, :, :], 1.0).then_inc(s["const_made"], 1)

            def layer_stats(n, which, nth, x=x_stream):
                raw, done = s[f"ln{which}_raw"], s[f"ln{which}_stats"]
                for i in range(T):
                    last = dve.bn_stats(stats[which][:, T * n.b + i], x[:, T * n.b + i])
                last.then_inc(raw, 1)
                dve.wait_ge(raw, nth)
                take_waits()
                for i in range(T):
                    last = dve.bn_aggr(meanvar[which][:, T * n.b + i], stats[which][:, T * n.b + i])
                last.then_inc(done, 1)

            def input_stats(b):
                dve.wait_ge(s[f"x{b}_in"], 16)
                for i in range(T):
                    last = dve.bn_stats(stats[0][:, T * b + i], x_in[:, T * b + i])
                last.then_inc(s["s0_raw"], 1)
                dve.wait_ge(s["s0_raw"], b + 1)
                for i in range(T):
                    last = dve.bn_aggr(meanvar[0][:, T * b + i], stats[0][:, T * b + i])
                last.then_inc(s["s0_mv"], 1)

            def input_norm(b):
                dve.wait_ge(s["s0_rstd"], b + 1)
                for c in range(T * b, T * b + T):
                    last = ts(x_norm[:, c], x_in[:, c], meanvar[0][:, c, 0:1], rstd[0][:, c:c + 1], ALU.subtract, ALU.mult)
                last.then_inc(s["x0_ready"], 1)
                dve.wait_ge(s["x0_ready"], b + 1)
                layer_stats(Turn(0, b), 1, b + 1, x_norm)

            for b in range(B):
                input_stats(b)
                if b:
                    input_norm(b - 1)
            input_norm(B - 1)
            dve.wait_ge(s["conv_in"], 32)
            dve.wait_ge(s["const_in"], 16)
            for g in range(2):
                last = ts(w_conv[:, g * G:(g + 1) * G], group, conv_col[:, g:g + 1], None, ALU.mult)
            last.then_inc(s["convw_made"], 1)
            ts(neg_hartley[:, :], hartley, -1.0, None, ALU.mult).then_inc(s["neg_made"], 1)
            dve.wait_ge(s["bias_in"], 9 * 16)
            ts(bias_parts[:, :], bias_rows[:, :], 1.0, None, ALU.mult).then_inc(s["bias_hi"], 1)
            dve.wait_ge(s["bias_hi"], 1)
            tt(bias_rest[:, :], bias_rows[:, :], bias_parts[:, :], ALU.subtract).then_inc(s["bias_rem"], 1)
            dve.wait_ge(s["bias_rem"], 1)
            ts(bias_parts[64:P, :], bias_rest[64:P, :], 1.0, None, ALU.mult).then_inc(s["bias_mid"], 1)
            dve.wait_ge(s["bias_mid"], 1)
            tt(bias_parts[96:P, :], bias_rest[96:P, :], bias_parts[96:P, :], ALU.subtract).then_inc(s["bias_lo"], 1)

            def rest_of_start():
                for b in range(B):
                    dve.wait_ge(s["conv_sb"], b + 1)
                    last = dve.bn_stats(bn_stats[:, b], conv_out[:, b * S:(b + 1) * S])
                last.then_inc(s["bn_raw"], 1)
                dve.wait_ge(s["bn_raw"], 1)
                dve.bn_aggr(bn_mv[:, :], bn_stats[:, :]).then_inc(s["bn_mv_r"], 1)
                dve.wait_ge(s["bn_rstd"], 1)
                tt(bn_sc[:, 1:2], bott[:, 1:2], bn_sc[:, 0:1], ALU.mult).then_inc(s["bn_scale_r"], 1)
                dve.wait_ge(s["bn_scale_r"], 1)
                tt(bn_sc[:, 2:3], bn_mv[:, 0:1], bn_sc[:, 1:2], ALU.mult).then_inc(s["bn_ms_r"], 1)
                dve.wait_ge(s["bn_ms_r"], 1)
                tt(bn_sc[:, 3:4], bott[:, 2:3], bn_sc[:, 2:3], ALU.subtract).then_inc(s["bn_shift"], 1)

            def whole_turns(n):
                dve.wait_ge(s["rounded"], n.through())
                stt(frac[:, :], frac[:, :], ROUND, turns[:, :], ALU.subtract, ALU.subtract).then_inc(s["fraced"], 1)

            def quaternions(engine, n):
                for j in "qk":
                    engine.wait_ge(s[j + "d_sb"], n.through())
                engine.wait_ge(s["cosined"], n.through())
                engine.wait_ge(s[f"rolled{n.par}"], n.pairs(32, 32))

            def taken(n, *terms):
                if not n.static or n.k:
                    for term in terms:
                        dve.wait_ge(s[term], n.through(1))

            def square_01(n):
                a, b = quat[:, n.par, :, 0], quat[:, n.par, :, 1]
                quaternions(dve, n)
                taken(n, "c0a_r", "c1b_r")
                tt(square01[:, :], a[:, 0:2], b[:, 0:2], ALU.mult).then_inc(s["sq01_r"], 1)

            def c23_first(n):
                a, b = quat[:, n.par, :, 0], quat[:, n.par, :, 1]
                quaternions(dve, n)
                taken(n, "tripled")
                tt(ps_c[:, 2:4], a[:, 0:1].broadcast_to((P, 2, S)), b[:, 2:4], ALU.mult).then_inc(s["c23a_r"], 1)

            def c0_first(n):
                dve.wait_ge(s["sq01_r"], n.through())
                taken(n, "tripled")
                tt(ps_c[:, 0], square01[:, 0], square01[:, 1], ALU.subtract).then_inc(s["c0a_r"], 1)

            def c1_first(n):
                dve.wait_ge(s["sq01_r"], n.through())
                taken(n, "tripled")
                dve.memset(ps_c[:, 1, 0:1], 0.0)
                tt(ps_c[:, 1, 1:S], square01[:, 0, 1:S], square01[:, 0, 0:S - 1], ALU.subtract).then_inc(s["c1a_r"], 1)

            def c23_second(n):
                dve.wait_ge(s["c23a_r"], n.through())
                dve.wait_ge(s["p20_r"], n.through())
                tt(ps_c[:, 2:4], ps_c[:, 2:4], prod_20[:, :], ALU.add).then_inc(s["c23b_r"], 1)

            def c1_second(n):
                dve.wait_ge(s["c1a_r"], n.through())
                tt(ps_c[:, 1], ps_c[:, 1], square01[:, 1], ALU.add).then_inc(s["c1b_r"], 1)

            def c0_second(n):
                dve.wait_ge(s["c0a_r"], n.through())
                dve.wait_ge(s["sq23_r"], n.through())
                tt(ps_c[:, 0], ps_c[:, 0], sum23[:, :], ALU.subtract).then_inc(s["c0_made"], 1)

            def c1_third(n):
                dve.wait_ge(s["c1b_r"], n.through())
                dve.wait_ge(s["p23_r"], n.through())
                tt(ps_c[:, 1], ps_c[:, 1], prod_23[:, 0], ALU.add).then_inc(s["c1c_r"], 1)

            def c1_last(n):
                dve.wait_ge(s["c1c_r"], n.through())
                tt(ps_c[:, 1], ps_c[:, 1], prod_23[:, 1], ALU.subtract).then_inc(s["c1_made"], 1)

            def c23_last(n):
                dve.wait_ge(s["c23b_r"], n.through())
                dve.wait_ge(s["crossed"], n.through())
                tt(ps_c[:, 2:4], ps_c[:, 2:4], cross[:, :], ALU.add).then_inc(s["c23_made"], 1)

            def triple_products(n):
                dve.wait_ge(s["vd_sb"], n.through())
                for made in ("c0_made", "c1_made", "c23_made"):
                    dve.wait_ge(s[made], n.through())
                if not n.static or n.k:
                    dve.wait_ge(s["spec_ps"], n.through(1))
                else:
                    dve.wait_ge(s["bias_lo"], 1)
                tt(triple[:, :], ps_c[:, :], quat[:, n.par, :, 2], ALU.mult).then_inc(s["tripled"], 1)

            def spectrum_gain(n):
                dve.wait_ge(s["spec_ps"], n.through())
                if not n.static or n.k:
                    dve.wait_ge(s["attn_ps"], n.through(1))
                tt(filtered[:, :], ps_spec[:, :], gain, ALU.mult).then_inc(s["filter_sb"], 1)

            out_tiles = ps_out[:, :].rearrange("p (t e) -> p t e", t=T)

            def add_attention(n):
                x = x_stream[:, n.tiles]
                if n.static and n.k == 0:
                    dve.wait_ge(s["x0_copied"], B * 16)
                dve.wait_ge(s["attn_ps"], n.through())
                tt(x, out_tiles, x, ALU.add).then_inc(s["x_mid"], 1)

            def stats_2(n):
                dve.wait_ge(s["x_mid"], n.through())
                layer_stats(n, 2, n.through())

            def add_mlp(n):
                x = x_stream[:, n.tiles]
                dve.wait_ge(s["mlp_ps"], n.through())
                tt(x, out_tiles, x, ALU.add).then_inc(s["x_ready"], 1)

            def stats_1(n):
                if not (n.static and n.layer == LAYERS - 1):
                    dve.wait_ge(s["x_ready"], n.through())
                    layer_stats(n, 1, n.through(-B))

            def finish(n):
                if n.static and n.layer == LAYERS - 1:
                    dve.wait_ge(s["x_ready"], n.through())
                    dve.wait_ge(s["acc_made"], T * n.b + T)
                    if n.b >= 2:
                        dve.wait_ge(s[f"out{n.par}_out"], 16)
                    tt(result[:, n.par], x_stream[:, n.tiles], x_in[:, n.tiles], ALU.add).then_inc(s["resulted"], 1)

            def take_top(i, r):
                if r:
                    dve.wait_ge(s[f"struck{r - 1}"], i.count(2, 2))
                else:
                    dve.wait_ge(s["lg_sb"], i.through())
                take_waits()
                for g in range(2):
                    dve.max(top[:, i.par, r, g], (left if r else logits)[:, i.par, g]).then_inc(s[f"topped{r}"], 1)

            def negate_max(i):
                dve.wait_ge(s["topped0"], i.count(2, 2))
                if not i.static or i.k >= 2:
                    dve.wait_ge(s["exped"], i.count(2, 2 - 4))
                ts(neg_max[:, i.par, :], top[:, i.par, 0, :, 0], -1.0, None, ALU.mult).then_inc(s["negmax_r"], 1)

            def strike(i, r):
                dve.wait_ge(s[f"topped{r}"], i.count(2, 2))
                take_waits()
                for g in range(2):
                    dve.match_replace(left[:, i.par, g], top[:, i.par, r, g], (left if r else logits)[:, i.par, g],
                                      SELECTED).then_inc(s[f"struck{r}"], 1)

            def keep(i):
                p = i.par
                dve.wait_ge(s["exped"], i.count(2, 2))
                dve.reciprocal(rsum[:, p, :], esum[:, p, :]).then_inc(s["rsum_r"], 1)
                dve.wait_ge(s["struck3"], i.count(2, 2))
                stt(kept[:, p], left[:, p], SELECTED, expd[:, p], ALU.is_equal, ALU.mult).then_inc(s["kept_r"], 1)
                dve.wait_ge(s["rsum_r"], i.through())
                dve.wait_ge(s["kept_r"], i.through())
                stt(sparse[:, p], kept[:, p, 1], rsum[:, p, 1:2], x_norm_flat[:, bass.ds((i.base * B + i.k) * E, E)], ALU.mult, ALU.mult).then_inc(s["sparsed"], 1)

            def ffn_add(i):
                p = i.par
                x = x_flat[:, bass.ds((i.base * B + i.k) * E, E)]
                dve.wait_ge(s["ffn_ps"], i.through())
                stt(branch[:, p], kept[:, p, 0], rsum[:, p, 0:1], ps_out[:, 0:E], ALU.mult, ALU.mult).then_inc(s["branched"], 1)
                dve.wait_ge(s["branched"], i.through())
                tt(x, ps_out[:, E:2 * E], branch[:, p], ALU.add).then_inc(s["acc_made"], 1)

            def slot(at):
                at(3, take_top, 0)
                at(3, c0_first)
                at(4, whole_turns)
                at(0, finish)
                at(3, strike, 0)
                at(3, negate_max)
                at(1, add_mlp)
                at(3, c0_second)
                at(1, stats_1)
                at(3, triple_products)
                at(4, square_01)
                at(2, strike, 2)
                at(4, c23_first)
                at(3, take_top, 1)
                at(4, c1_first)
                at(2, take_top, 3)
                at(4, c1_second)
                at(2, strike, 3)
                at(4, c1_third)
                at(3, strike, 1)
                at(2, keep)
                at(3, spectrum_gain)
                at(4, c23_second)
                at(4, c1_last)
                at(3, add_attention)
                at(3, stats_2)
                at(2, ffn_add)
                at(4, c23_last)
                at(3, take_top, 2)

            run_slots(dve, slot, rest_of_start, (square_01,))

        @block.gpsimd
        def _(pool):
            tt, ts = pool.tensor_tensor, pool.tensor_scalar
            pool.memset(eps_tile[:, :], EPS)
            pool.memset(zeros[:, :], 0.0)
            pool.memset(minus_half[:, :], -0.5)
            pool.drain()

            def inverse_std(which, b, name, nth):
                c = slice(T * b, T * b + T)
                pool.wait_ge(s[f"{name}_mv" if which == 0 else f"{name}_stats"], nth)
                tt(var_eps[which][:, c], meanvar[which][:, c, 1], eps_tile[:, :], ALU.add).then_inc(s[f"{name}_eps"], 1)
                pool.wait_ge(s[f"{name}_eps"], nth)
                tt(rstd[which][:, c], var_eps[which][:, c], minus_half[:, c], ALU.pow).then_inc(s[f"{name}_rstd"], 1)
                if which == 0:
                    return
                pool.wait_ge(s[f"{name}_rstd"], nth)
                tt(mean_rstd[which][:, c], meanvar[which][:, c, 0], rstd[which][:, c], ALU.mult).then_inc(s[f"{name}_mr"], 1)
                pool.wait_ge(s[f"{name}_mr"], nth)
                tt(shift[which][:, c], zeros[:, :], mean_rstd[which][:, c], ALU.subtract).then_inc(s[f"{name}_shift"], 1)

            def difference(n):
                pool.wait_ge(s["t1_sb"], n.through())
                if not n.static or n.k:
                    for j in "qkv":
                        pool.wait_ge(s[j + "d_ps"], n.through(1))
                tt(h_diff[:, 1:S], h1[:, 1:S], h1[:, 0:S - 1], ALU.subtract).then_inc(s["diffed"], 1)

            def pair(n):
                return quat[:, n.par, :, 0], quat[:, n.par, :, 1]

            def ready(n, taken=None):
                for j in "qk":
                    pool.wait_ge(s[j + "d_sb"], n.through())
                pool.wait_ge(s["cosined"], n.through())
                pool.wait_ge(s[f"rolled{n.par}"], n.pairs(32, 32))
                if taken and (not n.static or n.k):
                    pool.wait_ge(s[taken], n.through(1))

            def times_b0(n):
                a, b = pair(n)
                ready(n, "c23b_r")
                tt(prod_20[:, :], a[:, 2:4], b[:, 0:1].broadcast_to((P, 2, S)), ALU.mult).then_inc(s["p20_r"], 1)

            def square_23(n):
                a, b = pair(n)
                ready(n, "c0_made")
                tt(square23[:, :], a[:, 2:4], b[:, 2:4], ALU.mult).then_inc(s["sq23_raw"], 1)
                pool.wait_ge(s["sq23_raw"], n.through())
                tt(sum23[:, :], square23[:, 0], square23[:, 1], ALU.add).then_inc(s["sq23_r"], 1)

            def product_23(n):
                a, b = pair(n)
                ready(n, "c1_made")
                tt(prod_23[:, 0], a[:, 2], b[:, 3], ALU.mult)
                tt(prod_23[:, 1], a[:, 3], b[:, 2], ALU.mult).then_inc(s["p23_r"], 1)

            def cross_1a(n):
                a, b = pair(n)
                ready(n)
                if not n.static or n.k:
                    pool.wait_ge(s["crossed"], n.through(1))
                tt(cross_a[:, :], a[:, 1:2].broadcast_to((P, 2, S)), b[:, 2:4], ALU.mult).then_inc(s["crossa_r"], 1)

            def cross_1b(n):
                a, b = pair(n)
                ready(n)
                if not n.static or n.k:
                    pool.wait_ge(s["crossed"], n.through(1))
                tt(cross_b[:, :], a[:, 2:4], b[:, 1:2].broadcast_to((P, 2, S)), ALU.mult).then_inc(s["crossb_r"], 1)

            def cross_terms(n):
                pool.wait_ge(s["crossa_r"], n.through())
                pool.wait_ge(s["crossb_r"], n.through())
                if not n.static or n.k:
                    pool.wait_ge(s["c23_made"], n.through(1))
                tt(cross[:, 0], cross_b[:, 1], cross_a[:, 1], ALU.subtract)
                tt(cross[:, 1], cross_a[:, 0], cross_b[:, 0], ALU.subtract).then_inc(s["crossed"], 1)

            def rstd_1(n):
                if not (n.static and n.layer == LAYERS - 1):
                    inverse_std(1, n.b, "ln1", n.through(-B))

            def rstd_2(n):
                inverse_std(2, n.b, "ln2", n.through())

            for b in range(B):
                inverse_std(0, b, "s0", b + 1)
                if b:
                    inverse_std(1, b - 1, "ln1", b)
            inverse_std(1, B - 1, "ln1", B)
            def rest_of_start():
                pool.wait_ge(s["bn_mv_r"], 1)
                tt(bn_sc[:, 2:3], bn_mv[:, 1:2], eps_tile[0:2 * G, 0:1], ALU.add).then_inc(s["bn_eps_r"], 1)
                pool.wait_ge(s["bn_eps_r"], 1)
                tt(bn_sc[:, 0:1], bn_sc[:, 2:3], minus_half[0:2 * G, 0:1], ALU.pow).then_inc(s["bn_rstd"], 1)

            def slot(at):
                at(2, square_23)
                at(3, product_23)
                at(0, rstd_1)
                at(3, times_b0)
                at(3, cross_1a)
                at(3, cross_1b)
                at(4, difference)
                at(3, cross_terms)
                at(2, rstd_2)

            run_slots(pool, slot, rest_of_start, (cross_1b,))


_INS = (["L0_attn_" + n for n in ("x", "ln1_w", "ln1_b", "attn_w", "attn_b", "aproj_w", "aproj_b", "ln2_w", "ln2_b",
                                  "fc_w", "fc_b", "mproj_w", "mproj_b")]
        + ["L0_ffn_weight", "L0_ffn_bias"]
        + [f"L0_ffn_{g}_{n}" for g in ("so", "si") for n in ("conv_w", "conv_b", "gamma", "beta", "lin_w", "lin_b")])


def kernel(**inputs):
    import numpy as _np
    import concourse.bacc as _bacc
    from concourse import mybir as _mybir
    from concourse.bass_utils import run_bass_kernel_spmd as _run

    nc = _bacc.Bacc("TRN2", target_bir_lowering=False, num_devices=1)
    arrays, aps = {}, {}
    for name in _INS:
        a = _np.ascontiguousarray(inputs[name])
        arrays[f"in_{name}_dram"] = a
        aps[name] = nc.dram_tensor(f"in_{name}_dram", a.shape, _mybir.dt.from_np(a.dtype), kind="ExternalInput").ap()
    c = shape_constants()
    arrays["shape_constants_dram"] = c
    consts = nc.dram_tensor("shape_constants_dram", c.shape, _mybir.dt.float32, kind="ExternalInput").ap()
    out = nc.dram_tensor("out_0_dram", (B, S, E), _mybir.dt.float32, kind="ExternalOutput").ap()
    build(nc, aps, consts, out)
    r = _run(nc, [arrays], core_ids=[0])
    return r.results[0]["out_0_dram"]
```
